# Optimizing a Trainium2 kernel written in Bass

```python
import numpy as np
import jax
import jax.numpy as jnp

def _softmax(x, axis=-1):
    return jax.nn.softmax(x, axis=axis)

def _gelu(x):
    return jax.nn.gelu(x, approximate=True)

def _silu(x):
    return jax.nn.silu(x)

def _sigmoid(x):
    return jax.nn.sigmoid(x)

def _layernorm(x, axis=-1, eps=1e-05):
    m = jnp.mean(x, axis=axis, keepdims=True)
    v = jnp.var(x, axis=axis, keepdims=True)
    return (x - m) / jnp.sqrt(v + eps)

def _scatter_add(tgt, idx, src, axis=0):
    return tgt.at[idx].add(src)

def _segment_sum(src, seg, n):
    return jax.ops.segment_sum(src, seg, n)
kernel_name = 'mk_decoder_postln_d1_seqx_r8_ec508d'

def setup_inputs(seed: int=0):
    np.random.seed(seed)
    _w = jnp.asarray

    def _rec_inputs():
        import jax
        import jax.numpy as jnp
        _rk = jax.random.key(seed)
        x = 0.0003765 + 1 * jax.random.normal(jax.random.fold_in(_rk, 1), (32, 128, 128), jnp.float32)
        _lenS = 128 - jax.random.randint(jax.random.fold_in(_rk, 7), (32,), 0, max(1, 128 // 4) + 1, jnp.int32)
        _lenS2 = 77 - jax.random.randint(jax.random.fold_in(_rk, 8), (32,), 0, max(1, 77 // 4) + 1, jnp.int32)
        _ctx_1024P = jax.random.normal(jax.random.fold_in(_rk, 11), (32, 16, 128), jnp.float32)
        _ctx_1024c = jax.random.dirichlet(jax.random.fold_in(_rk, 511), 0.3 * jnp.ones((16,), jnp.float32), (32, 77))
        _ctx_1024t = jnp.einsum('bsk,bkd->bsd', _ctx_1024c, _ctx_1024P)
        _ctx_1024t = _ctx_1024t * jax.lax.rsqrt(jnp.mean(jnp.square(_ctx_1024t)) + 1e-12) * 0.953939
        ctx_1024 = -0.000292821 + 1.00034 * (_ctx_1024t + 0.3 * jax.random.normal(jax.random.fold_in(_rk, 611), (32, 77, 128), jnp.float32))
        _validS = jnp.arange(128)[None, :] < _lenS[:, None]
        _validS2 = jnp.arange(77)[None, :] < _lenS2[:, None]
        _causal = jnp.tril(jnp.ones((128, 128), dtype=bool))
        mask_1x1xSxS2_fk1 = jnp.where(jnp.broadcast_to(_validS2[0:1, None, None, :], (1, 1, 128, 77)), 1.0, 0.0).astype(jnp.float32)
        return (x, ctx_1024, mask_1x1xSxS2_fk1)
    x, ctx_1024, mask_1x1xSxS2_fk1 = _rec_inputs()

    def _L0_attn_setup():
        import jax, jax.numpy as jnp
        import numpy as np
        DIM = 128
        HEADS = 16
        DIM_HEAD = 64
        SOFTCAP = 50.0
        key = jax.random.key(seed)
        k1, k2, k3, k4 = jax.random.split(key, 4)
        b, n = (2, 256)
        dim_inner = HEADS * DIM_HEAD
        x = jax.random.normal(k1, (b, n, DIM), dtype=jnp.float32)
        w_qkv = jax.random.normal(k2, (DIM, 3 * dim_inner), dtype=jnp.float32) * 0.02
        w_gates = jax.random.normal(k3, (DIM, HEADS), dtype=jnp.float32) * 0.02
        w_out = jax.random.normal(k4, (dim_inner, DIM), dtype=jnp.float32) * 0.02
        return {'x': x, 'w_qkv': w_qkv, 'w_gates': w_gates, 'w_out': w_out}
    _L0_attn_all = _L0_attn_setup()
    _L0_attn_in = {k: v for k, v in _L0_attn_all.items() if k in ('w_qkv', 'w_gates', 'w_out')}
    del _L0_attn_all

    def _L0_xattn_setup():
        import jax, jax.numpy as jnp
        import numpy as np
        B, S, E, H = (2, 256, 128, 16)
        D = E // H

        def _split_heads(x):
            b, s, _ = x.shape
            return x.reshape(b, s, H, D).transpose(0, 2, 1, 3)
        key = jax.random.key(seed)
        ks = jax.random.split(key, 12)
        scale = 1.0 / np.sqrt(E)
        inp = {'v': jax.random.normal(ks[0], (B, S, E), jnp.float32), 'k': jax.random.normal(ks[1], (B, S, E), jnp.float32), 'q': jax.random.normal(ks[2], (B, S, E), jnp.float32), 'mask': jnp.triu(jnp.ones((S, S), jnp.float32), k=1)[None, None, :, :], 'wq': jax.random.normal(ks[3], (E, E), jnp.float32) * scale, 'bq': jnp.zeros((E,), jnp.float32), 'wk': jax.random.normal(ks[4], (E, E), jnp.float32) * scale, 'bk': jnp.zeros((E,), jnp.float32), 'wv': jax.random.normal(ks[5], (E, E), jnp.float32) * scale, 'bv': jnp.zeros((E,), jnp.float32), 'wo': jax.random.normal(ks[6], (E, E), jnp.float32) * scale, 'bo': jnp.zeros((E,), jnp.float32)}
        return inp
    _L0_xattn_all = _L0_xattn_setup()
    _L0_xattn_in = {k: v for k, v in _L0_xattn_all.items() if k in ('wq', 'bq', 'wk', 'bk', 'wv', 'bv', 'wo', 'bo')}
    del _L0_xattn_all

    def _L0_ffn_setup():
        import jax, jax.numpy as jnp
        import numpy as np
        B, S, D, E, F = (2, 256, 128, 8, 512)
        key = jax.random.key(seed)
        ks = jax.random.split(key, 4)
        return {'hidden_states': jax.random.normal(ks[0], (B, S, D), dtype=jnp.float32), 'Wr': jax.random.normal(ks[1], (D, E), dtype=jnp.float32) * (1.0 / np.sqrt(D)), 'W1': jax.random.normal(ks[2], (E, D, F), dtype=jnp.float32) * (1.0 / np.sqrt(D)), 'b1': jnp.zeros((E, F), dtype=jnp.float32), 'W2': jax.random.normal(ks[3], (E, F, D), dtype=jnp.float32) * (1.0 / np.sqrt(F)), 'b2': jnp.zeros((E, D), dtype=jnp.float32)}
    _L0_ffn_all = _L0_ffn_setup()
    _L0_ffn_in = {k: v for k, v in _L0_ffn_all.items() if k in ('Wr', 'W1', 'b1', 'W2', 'b2')}
    del _L0_ffn_all
    return {'x': x, 'ctx_1024': ctx_1024, 'mask_1x1xSxS2_fk1': mask_1x1xSxS2_fk1, 'L0_attn_w_qkv': _L0_attn_in['w_qkv'], 'L0_attn_w_gates': _L0_attn_in['w_gates'], 'L0_attn_w_out': _L0_attn_in['w_out'], 'L0_xattn_wq': _L0_xattn_in['wq'], 'L0_xattn_bq': _L0_xattn_in['bq'], 'L0_xattn_wk': _L0_xattn_in['wk'], 'L0_xattn_bk': _L0_xattn_in['bk'], 'L0_xattn_wv': _L0_xattn_in['wv'], 'L0_xattn_bv': _L0_xattn_in['bv'], 'L0_xattn_wo': _L0_xattn_in['wo'], 'L0_xattn_bo': _L0_xattn_in['bo'], 'L0_ffn_Wr': _L0_ffn_in['Wr'], 'L0_ffn_W1': _L0_ffn_in['W1'], 'L0_ffn_b1': _L0_ffn_in['b1'], 'L0_ffn_W2': _L0_ffn_in['W2'], 'L0_ffn_b2': _L0_ffn_in['b2']}

def reference(x, ctx_1024, mask_1x1xSxS2_fk1, L0_attn_w_qkv, L0_attn_w_gates, L0_attn_w_out, L0_xattn_wq, L0_xattn_bq, L0_xattn_wk, L0_xattn_bk, L0_xattn_wv, L0_xattn_bv, L0_xattn_wo, L0_xattn_bo, L0_ffn_Wr, L0_ffn_W1, L0_ffn_b1, L0_ffn_W2, L0_ffn_b2):
    import jax
    import jax.numpy as jnp

    def _L0_attn_ref(x, w_qkv, w_gates, w_out):
        import jax, jax.numpy as jnp
        import numpy as np
        DIM = 128
        HEADS = 16
        DIM_HEAD = 64
        SOFTCAP = 50.0
        b, n, _ = x.shape
        scale = DIM_HEAD ** (-0.5)
        qkv = jnp.einsum('bnf,fe->bne', x, w_qkv).reshape(b, n, 3, HEADS, DIM_HEAD)
        qkv = jnp.moveaxis(qkv, 2, 0)
        q, k, v = jnp.moveaxis(qkv, 3, 2)
        q = q * scale
        sim = jnp.einsum('bhid,bhjd->bhij', q, k)
        sim = SOFTCAP * jnp.tanh(sim / SOFTCAP)
        mask_value = -jnp.finfo(sim.dtype).max
        causal_mask = jnp.triu(jnp.ones((n, n), dtype=bool), 1)
        sim = jnp.where(causal_mask, mask_value, sim)
        attn = jax.nn.softmax(sim, axis=-1)
        out = jnp.einsum('bhij,bhjd->bhid', attn, v)
        gates = jax.nn.sigmoid(jnp.einsum('bnf,fh->bhn', x, w_gates))[..., None]
        out = out * gates
        out = jnp.transpose(out, (0, 2, 1, 3)).reshape(b, n, HEADS * DIM_HEAD)
        return jnp.einsum('bne,ef->bnf', out, w_out)

    def _L0_xattn_ref(v, k, q, mask, wq, bq, wk, bk, wv, bv, wo, bo):
        import jax, jax.numpy as jnp
        import numpy as np
        B, S, E, H = (2, 256, 128, 16)
        D = E // H

        def _split_heads(x):
            b, s, _ = x.shape
            return x.reshape(b, s, H, D).transpose(0, 2, 1, 3)
        qh = _split_heads(q @ wq + bq)
        kh = _split_heads(k @ wk + bk)
        vh = _split_heads(v @ wv + bv)
        logits = jnp.einsum('bhqd,bhkd->bhqk', qh, kh) / jnp.sqrt(jnp.float32(D))
        logits = logits + mask * -1000000000.0
        attn = jax.nn.softmax(logits, axis=-1)
        out = jnp.einsum('bhqk,bhkd->bhqd', attn, vh)
        out = out.transpose(0, 2, 1, 3).reshape(q.shape[0], -1, E)
        return out @ wo + bo

    def _L0_ffn_ref(hidden_states, Wr, W1, b1, W2, b2):
        import jax, jax.numpy as jnp
        import numpy as np
        B, S, D, E, F = (2, 256, 128, 8, 512)
        b, s, d = hidden_states.shape
        e = Wr.shape[1]
        x = hidden_states.reshape(b * s, d)
        router_logits = x @ Wr
        router_probs = jax.nn.softmax(router_logits, axis=-1)
        expert_idx = jnp.argmax(router_probs, axis=-1)
        p_max = jnp.max(router_probs, axis=-1, keepdims=True)

        def expert_mlp(w1, bb1, w2, bb2):
            h = jax.nn.gelu(x @ w1 + bb1, approximate=False)
            return h @ w2 + bb2
        outs = jax.vmap(expert_mlp)(W1, b1, W2, b2)
        onehot = jax.nn.one_hot(expert_idx, e, dtype=x.dtype)
        next_states = jnp.einsum('te,etd->td', onehot, outs)
        out = p_max * next_states
        return out.reshape(b, s, d)
    x = _layernorm(x + _L0_attn_ref(x, L0_attn_w_qkv, L0_attn_w_gates, L0_attn_w_out), axis=-1)
    x = _layernorm(x + _L0_xattn_ref(ctx_1024, ctx_1024, x, mask_1x1xSxS2_fk1, L0_xattn_wq, L0_xattn_bq, L0_xattn_wk, L0_xattn_bk, L0_xattn_wv, L0_xattn_bv, L0_xattn_wo, L0_xattn_bo), axis=-1)
    x = _layernorm(x + _L0_ffn_ref(x, L0_ffn_Wr, L0_ffn_W1, L0_ffn_b1, L0_ffn_W2, L0_ffn_b2), axis=-1)
    return x

_drawn_inputs = setup_inputs


def setup_inputs(seed=0):
    import zlib

    import numpy as np

    out = dict(_drawn_inputs(seed))
    spreads = {'L0_xattn_bq': (0.0, 0.1),
     'L0_xattn_bk': (0.0, 0.8),
     'L0_xattn_bv': (0.0, 0.1),
     'L0_xattn_bo': (0.0, 0.1),
     'L0_ffn_b1': (0.0, 0.325),
     'L0_ffn_b2': (0.0, 0.1)}
    factors = {'L0_attn_w_qkv': 2.669, 'L0_attn_w_gates': 8.0}
    for name, (base, spread) in spreads.items():
        noise = np.random.default_rng([zlib.crc32(name.encode()), seed]).standard_normal(out[name].shape)
        drawn = base * np.exp(spread * noise) if base else spread * noise
        out[name] = jnp.asarray(drawn.astype(out[name].dtype))
    for name, factor in factors.items():
        out[name] = (out[name] * factor).astype(out[name].dtype)
    return out
```

```python
from contextlib import ExitStack

import concourse.bass as bass
from concourse import mybir

ALU = mybir.AluOpType
ACT = mybir.ActivationFunctionType
AX = mybir.AxisListType
F32 = mybir.dt.float32
BF16 = mybir.dt.bfloat16
I32 = mybir.dt.int32

P = 128
B = 32
H, DH = 16, 64
INNER = H * DH
NCH = INNER // P
SOFTCAP = 50.0
S2 = 77
XD = P // H
NE, FF = 8, 512
NFC = FF // P
REGION = B * P + P
NT = 40
ROW = P + 4
PROB, TOKEN = P, P + 1
NOBODY = 8000.0
EPS = 1e-5
HEAD_W = DH + 1


def head_of(wave, k):
    return 8 * (wave // 2) + 2 * k + wave % 2


class Chain:

    def __init__(self, eng, sem, per):
        self.eng, self.sem, self.per = eng, sem, per

    def start(self, batch):
        self.base, self.k = batch * self.per, 0

    def link(self, ins):
        self.k += 1
        ins.then_inc(self.sem, 1)
        self.eng.wait_ge(self.sem, self.base + self.k)

    def end(self):
        assert self.k == self.per, (self.k, self.per)


def at_least(eng, sem, value):
    if not isinstance(value, int) or value > 0:
        eng.wait_ge(sem, value)


def has(n, low, high):
    return not isinstance(n, int) or low <= n <= high


def run_steps(eng, step, early=lambda: None):
    step(-1, 1)
    step(0, 0)
    step(0, 1)
    early()
    step(1, 0)
    step(1, 1)
    with eng.Fori(2, B // 2 - 1) as i:
        step(i, 0)
        step(i, 1)
    for i in (B // 2 - 1, B // 2):
        step(i, 0)
        step(i, 1)


def decoder_layer(nc, x, xT, ctxT, mask, w_qkv, w_gates, w_out, wq, bq, wk, bk, wv, bv, wo, bo,
                  Wr, W1, b1, W2, b2, out):
    out_rows = out.rearrange("b s d -> (b s) d")
    scratch = nc.dram_tensor("scratch", [NE * REGION + P, ROW], F32, kind="Internal").ap()

    with ExitStack() as ctx:
        def sb(name, shape, dt=F32):
            return ctx.enter_context(nc.sbuf_tensor(name, shape, dt))

        def sem(name):
            return ctx.enter_context(nc.semaphore(name))

        ps = ctx.enter_context(nc.psum_tensor("ps", [P, 8, 512], F32))

        wqkv_sb = sb("wqkv_sb", [P, 3 * INNER])
        wg_sb = sb("wg_sb", [P, H])
        wout_sb = sb("wout_sb", [P, NCH, P])
        wq_sb, wk_sb, wv_sb, wo_sb = (sb(f"{w}_sb", [P, P]) for w in ("wq", "wk", "wv", "wo"))
        bq_sb, bk_sb = sb("bq_sb", [P, 1]), sb("bk_sb", [P, 1])
        bv_sb, bo_sb = sb("bv_sb", [S2, P]), sb("bo_sb", [P, P])
        wr_sb = sb("wr_sb", [P, NE])
        w1_sb = sb("w1_sb", [P, NE * FF])
        w2_sb = sb("w2_sb", [P, NE * NFC * P])
        mask_sb = sb("mask_sb", [P, S2])
        ident = sb("ident", [P, P])
        before = sb("before", [P, P])
        ones = sb("ones", [P, P])
        head_rows = sb("head_rows", [P, H])
        in_group = sb("in_group", [P, 4])
        ones_exp = sb("ones_exp", [S2, 4, 32])
        falling = sb("falling", [P, NE])
        region_of = sb("region_of", [P, NE])
        half_neg = sb("half_neg", [P, 2])

        xT_sb = [sb(f"xT_sb{u}", [P, P]) for u in range(2)]
        x_sb = [sb(f"x_sb{u}", [P, P]) for u in range(2)]
        ctx_sb = [sb(f"ctx_sb{u}", [P, S2]) for u in range(2)]
        qT = [sb(f"qT{u}", [P, NCH, P]) for u in range(2)]
        kT = [sb(f"kT{u}", [P, NCH, P]) for u in range(2)]
        v1 = [sb(f"v1{u}", [P, H, HEAD_W]) for u in range(2)]
        probs = [sb(f"probs{g}", [P, 4, P]) for g in range(4)]
        gate_z, gate_e, gate_1, gate = (sb(f"gate_{s}", [P, H]) for s in ("z", "e", "1", "g"))
        rsum = sb("rsum", [P, 2, 4])
        rgate = sb("rgate", [P, 2, 4])
        attn = sb("attn", [P, INNER])
        attnT = sb("attnT", [P, NCH, P])
        y1 = sb("y1", [P, P])
        y2 = sb("y2", [P, P])
        bn = sb("bn", [P, 2, 6])
        mv = sb("mv", [P, 2, 2])
        var_eps = sb("var_eps", [P, 2])
        rstd = sb("rstd", [P, 2])
        x1 = [sb(f"x1_{u}", [P, P]) for u in range(2)]
        x1_bo = sb("x1_bo", [P, P])
        x1T = sb("x1T", [P, P])
        q1T = sb("q1T", [P, P])
        k_exp = sb("k_exp", [P, 4, S2])
        v_exp = sb("v_exp", [S2, H, 32])
        logits = sb("logits", [P, H, S2])
        lmax = sb("lmax", [P, H])
        xprobsT = sb("xprobsT", [S2, H, P])
        xrec = sb("xrec", [P, P])
        xattnT = sb("xattnT", [P, P])
        row = [sb(f"row{u}", [P, ROW]) for u in range(2)]
        x2T = sb("x2T", [P, P])
        r_max = sb("r_max", [P, 1])
        r_low = sb("r_low", [P, NE])
        r_exp = sb("r_exp", [P, NE])
        r_sum = sb("r_sum", [P, 1])
        r_key = sb("r_key", [P, NE])
        r_first = sb("r_first", [P, 1])
        one_hot = sb("one_hot", [P, NE])
        counted = sb("counted", [P, NE])
        r_pos = sb("r_pos", [P, NE])
        pos_f = sb("pos_f", [P, 1])
        pos_i = [sb(f"pos_i{u}", [P, 1], I32) for u in range(2)]

        tail = sb("tail", [P, NE])
        n_rows = sb("n_rows", [P, NE])
        n_tiles_i = sb("n_tiles_i", [P, NE], I32)
        n_tiles = sb("n_tiles", [P, NE])
        tile_end = sb("tile_end", [P, NE])
        part_f = sb("part_f", [P, 1])
        tail_i = sb("tail_i", [P, NE], I32)
        tile_no = sb("tile_no", [1, NT + 1, NE])
        past = sb("past", [1, NT + 1, NE])
        t_exp, t_start, t_row = (sb(f"t_{s}", [1, NT + 1]) for s in ("exp", "start", "row"))
        row_at = sb("row_at", [1, NT + 1], I32)
        exp_at = sb("exp_at", [1, NT + 1], I32)
        nobody_row = sb("nobody_row", [P, ROW])

        b_in = [sb("b1_in", [P, NE * FF // P]), sb("b2_in", [P, NE])]
        b_rest = [sb("b1_rest", [P, NE * FF // P]), sb("b2_rest", [P, NE])]
        b_part = [[sb(f"b{w + 1}_part{k}", [P, n], BF16) for k in range(3)] for w, n in enumerate((NE * FF // P, NE))]
        b1_3 = sb("b1_3", [3, NE * FF], BF16)
        b2_3 = sb("b2_3", [3, NE * P], BF16)
        ones_3 = sb("ones_3", [3, P], BF16)
        trow = [sb(f"trow{k}", [P, ROW]) for k in range(4)]
        xeT = [sb(f"xeT{k}", [P, P]) for k in range(2)]
        hid = [sb(f"hid{k}", [P, FF]) for k in range(2)]
        hidT = [sb(f"hidT{k}", [P, NFC, P]) for k in range(2)]
        y3 = [sb(f"y3_{k}", [P, P]) for k in range(2)]
        bn3 = sb("bn3", [P, 6])
        mv3 = [sb(f"mv3_{k}", [P, 2]) for k in range(2)]
        var3 = sb("var3", [P, 1])
        rstd3 = [sb(f"rstd3_{k}", [P, 1]) for k in range(2)]
        x3 = [sb(f"x3_{k}", [P, P]) for k in range(4)]
        tok_i = [sb(f"tok_i{k}", [P, 1], I32) for k in range(4)]

        first_w, other_w, ffn_w, b_loaded = sem("first_w"), sem("other_w"), sem("ffn_w"), sem("b_loaded")
        xT_loaded = [sem(f"xT_loaded{u}") for u in range(2)]
        x_loaded = [sem(f"x_loaded{u}") for u in range(2)]
        ctx_loaded = [sem(f"ctx_loaded{u}") for u in range(2)]
        pool_const, dve_const = sem("pool_const"), sem("dve_const")
        proj_ready, qk_kept, v_kept = sem("proj_ready"), sem("qk_kept"), sem("v_kept")
        scores_ready, tanh_done, exp_done, causal_done = (
            sem("scores_ready"), sem("tanh_done"), sem("exp_done"), sem("causal_done"))
        av_ready, attn_kept = sem("av_ready"), sem("attn_kept")
        attnT_ready, attnT_kept = sem("attnT_ready"), sem("attnT_kept")
        y_ready, y_kept = sem("y_ready"), sem("y_kept")
        gate_exp_done = sem("gate_exp_done")
        stats_done, rstd_done = sem("stats_done"), sem("rstd_done")
        x1_done, x1_bo_done, x2_done = sem("x1_done"), sem("x1_bo_done"), sem("x2_done")
        x1T_ready, x1T_kept = sem("x1T_ready"), sem("x1T_kept")
        qkv1_ready, qkv1_kept = sem("qkv1_ready"), sem("qkv1_kept")
        xscores_ready, xscores_kept = sem("xscores_ready"), sem("xscores_kept")
        shifted, xexp_done = sem("shifted"), sem("xexp_done")
        xpT_ready, xpT_kept = sem("xpT_ready"), sem("xpT_kept")
        xav_ready, xattnT_kept = sem("xav_ready"), sem("xattnT_kept")
        y2_ready, y2_kept = sem("y2_ready"), sem("y2_kept")
        x2T_ready, x2T_kept = sem("x2T_ready"), sem("x2T_kept")
        router_ready, router_kept, r_exp_done = sem("router_ready"), sem("router_kept"), sem("r_exp_done")
        one_hot_done, place_ready, place_kept = sem("one_hot_done"), sem("place_ready"), sem("place_kept")
        row_done = sem("row_done")
        scattered = [sem(f"scattered{u}") for u in range(2)]
        dve_s, dve_x, dve_r, dve_t = sem("dve_s"), sem("dve_x"), sem("dve_r"), sem("dve_t")
        pool_ln = sem("pool_ln")
        pool_passed, dve_passed = sem("pool_passed"), sem("dve_passed")
        count_ready, tail_done, tails_written, table_done = (
            sem("count_ready"), sem("tail_done"), sem("tails_written"), sem("table_done"))
        b_split, b_placed = sem("b_split"), sem("b_placed")
        trow_loaded = [sem(f"trow_loaded{k}") for k in range(4)]
        xeT_ready, xeT_kept = sem("xeT_ready"), sem("xeT_kept")
        hid_ready, gelu_done = sem("hid_ready"), sem("gelu_done")
        hidT_ready, hidT_kept = sem("hidT_ready"), sem("hidT_kept")
        y3_ready, y3_kept = sem("y3_ready"), sem("y3_kept")
        stats3_done, rstd3_done, x3_done, pool_3, dve_3 = (
            sem("stats3_done"), sem("rstd3_done"), sem("x3_done"), sem("pool_3"), sem("dve_3"))
        out_written = [sem(f"out_written{k}") for k in range(4)]

        N_FIRST, N_OTHER, N_FFN = 3, 10, 2
        N_POOL_CONST = 26
        wqkv_v = wqkv_sb[:, :].rearrange("p (s e) -> p s e", s=3)

        block = ctx.enter_context(nc.Block())

        @block.sync
        def _(sp):
            def load_batch(i, u):
                b = 2 * i + u
                if not (isinstance(b, int) and b < 2):
                    at_least(sp, y_ready, b - 1)
                sp.dma_start(xT_sb[u][:], xT[:, bass.ds(b * P, P)]).then_inc(xT_loaded[u], 16)
                at_least(sp, qkv1_ready, b - 1)
                sp.dma_start(ctx_sb[u][:], ctxT[:, bass.ds(b * S2, S2)]).then_inc(ctx_loaded[u], 16)
                if not (isinstance(b, int) and b < 2):
                    at_least(sp, y_kept, b)
                sp.dma_start(x_sb[u][:], x[bass.ds(b * P, P), :]).then_inc(x_loaded[u], 16)

            sp.dma_start(wqkv_sb[:], w_qkv).then_inc(first_w, 16)
            sp.dma_start(xT_sb[0][:], xT[:, 0:P]).then_inc(xT_loaded[0], 16)
            sp.dma_start(wg_sb[:], w_gates).then_inc(first_w, 16)
            sp.dma_start(wout_sb[:], w_out.rearrange("(c p) d -> p c d", p=P)).then_inc(first_w, 16)
            sp.dma_start(xT_sb[1][:], xT[:, P:2 * P]).then_inc(xT_loaded[1], 16)
            for u in range(2):
                sp.dma_start(ctx_sb[u][:], ctxT[:, u * S2:(u + 1) * S2]).then_inc(ctx_loaded[u], 16)
                sp.dma_start(x_sb[u][:], x[u * P:(u + 1) * P, :]).then_inc(x_loaded[u], 16)
            for dst, src in ((wq_sb, wq), (wk_sb, wk), (wv_sb, wv), (wo_sb, wo), (bq_sb, bq), (bk_sb, bk),
                             (wr_sb, Wr), (mask_sb, mask)):
                sp.dma_start(dst[:], src).then_inc(other_w, 16)
            sp.dma_start(bv_sb[:], bv.partition_broadcast(S2)).then_inc(other_w, 16)
            sp.dma_start(bo_sb[:], bo.partition_broadcast(P)).then_inc(other_w, 16)
            sp.dma_start(b_in[0][:], b1.rearrange("e (q f) -> (e q) f", q=P // NE)).then_inc(b_loaded, 16)
            sp.dma_start(b_in[1][:], b2.rearrange("e (q f) -> (e q) f", q=P // NE)).then_inc(b_loaded, 16)
            sp.dma_start(w1_sb[:, :].rearrange("p (e f) -> p e f", e=NE),
                         W1.rearrange("e d f -> d e f")).then_inc(ffn_w, 16)
            sp.dma_start(w2_sb[:, :].rearrange("p (e c d) -> p e c d", e=NE, c=NFC),
                         W2.rearrange("e (c p) d -> p e c d", p=P)).then_inc(ffn_w, 16)
            with sp.Fori(1, B // 2) as i:
                load_batch(i, 0)
                load_batch(i, 1)

            sp.wait_ge(b_split, 1)
            for w, dst in enumerate((b1_3, b2_3)):
                for k in range(3):
                    sp.dma_start(dst[k:k + 1, :], b_part[w][k][:]).then_inc(b_placed, 16)

            sp.wait_ge(table_done, 2)
            sp.wait_ge(tails_written, 16 * (NE + 1))
            sp.wait_ge(scattered[0], 16 * (B // 2))
            sp.wait_ge(scattered[1], 16 * (B // 2))

            def load_tile(jj, k):
                start = sp.value_load(row_at[0:1, bass.ds(4 * jj + k, 1)], min_val=0, max_val=NE * REGION)
                at_least(sp, stats3_done, 4 * jj + k - 3)
                sp.dma_start(trow[k][:], scratch[bass.ds(start, P), :]).then_inc(trow_loaded[k], 16)

            for k in range(4):
                load_tile(0, k)
            with sp.Fori(1, NT // 4) as jj:
                for k in range(4):
                    load_tile(jj, k)
            for k in range(4):
                sp.wait_ge(out_written[k], 16 * (NT // 4))

        @block.gpsimd
        def _(pool):
            def select(out_ap, in_ap, pattern, op, base=0, cm=0, fill=0.0):
                return pool.affine_select(out=out_ap, in_=in_ap, pattern=pattern, compare_op=op,
                                          fill=fill, base=base, channel_multiplier=cm)

            count = [0]

            def const(ins):
                ins.then_inc(pool_const, 1)
                count[0] += 1

            def settle():
                pool.wait_ge(pool_const, count[0])

            for t in (ones, ident, before, head_rows, ones_exp):
                const(pool.memset(t[:], 1.0))
            const(pool.memset(v_exp[:], 0.0))
            const(pool.memset(half_neg[:], -0.5))
            const(pool.iota(falling[:], [[-1, NE]], base=NE, channel_multiplier=0,
                            allow_small_or_imprecise_dtypes=True))
            const(pool.iota(region_of[:], [[REGION, NE]], base=0, channel_multiplier=0,
                            allow_small_or_imprecise_dtypes=True))
            const(pool.iota(part_f[:], [[0, 1]], base=0, channel_multiplier=1,
                            allow_small_or_imprecise_dtypes=True))
            const(pool.iota(tile_no[:], [[1, NT + 1], [0, NE]], base=0, channel_multiplier=0,
                            allow_small_or_imprecise_dtypes=True))
            const(pool.memset(nobody_row[:], 0.0))
            for u in range(2):
                const(pool.memset(v1[u][:, :, DH:HEAD_W], 1.0))
                const(pool.memset(row[u][:], 0.0))
            settle()
            const(select(ident[:], ident[:], [[-1, P]], ALU.is_equal, cm=1))
            const(select(before[:], before[:], [[1, P]], ALU.is_gt, cm=-1))
            const(select(head_rows[:], head_rows[:], [[-XD, H]], ALU.is_ge, cm=1))
            const(select(ones_exp[:], ones_exp[:], [[-XD, 4], [1, 32]], ALU.is_ge))
            const(select(counted[:], region_of[:], [[0, NE]], ALU.is_equal, cm=1))
            const(pool.memset(nobody_row[:, TOKEN:TOKEN + 1], NOBODY))
            for u in range(2):
                const(pool.iota(row[u][:, TOKEN:TOKEN + 1], [[0, 1]], base=(u - 2) * P, channel_multiplier=1,
                                allow_small_or_imprecise_dtypes=True))
            settle()
            const(select(head_rows[:], head_rows[:], [[XD, H]], ALU.is_ge, base=XD - 1, cm=-1))
            const(select(ones_exp[:], ones_exp[:], [[XD, 4], [-1, 32]], ALU.is_ge, base=XD - 1))
            assert count[0] == N_POOL_CONST
            settle()
            pool.dma_start(scratch[NE * REGION:NE * REGION + P, :], nobody_row[:]).then_inc(tails_written, 16)

            def take_wait():
                pool.sem_inc(pool_passed, 1)

            def step(i, u):
                n = 2 * i + u
                m, r = n - 1, n - 2

                def causal(g):
                    at_least(pool, exp_done, 4 * n + g + 1)
                    take_wait()
                    select(probs[g][:], probs[g][:], [[0, 4], [1, P]], ALU.is_ge, cm=-1).then_inc(causal_done, 1)

                if has(n, 1, B):
                    at_least(pool, x1_done, m + 1)
                    take_wait()
                    pool.tensor_tensor(x1_bo[:], x1[1 - u][:], bo_sb[:], ALU.add).then_inc(x1_bo_done, 1)
                if has(n, 0, B - 1):
                    causal(0)
                    causal(1)
                    causal(2)
                    causal(3)
                if has(n, 2, B + 1):
                    at_least(pool, row_done, r + 1)
                    take_wait()
                    pool.indirect_dma_start(scratch[0:NE * REGION, :], bass.IndirectOffsetOnAxis(pos_i[u][:, 0:1], 0),
                                            row[u][:], None).then_inc(scattered[u], 16)
                if has(n, 0, B):
                    a, z = (0 if has(n, 0, B - 1) else 1), (2 if has(n, 1, B) else 1)
                    at_least(pool, stats_done, 2 * n + 1 if has(n, 0, B - 1) else 2 * B)
                    take_wait()
                    pool.tensor_scalar(var_eps[:, a:z], mv[:, a:z, 1], EPS, None, ALU.add).then_inc(pool_ln, 1)
                    pool.wait_ge(pool_ln, n + 1)
                    take_wait()
                    pool.tensor_tensor(rstd[:, a:z], var_eps[:, a:z], half_neg[:, a:z], ALU.pow).then_inc(rstd_done, 1)

            pool.wait_ge(other_w, 16 * N_OTHER)
            run_steps(pool, step)

            pool.wait_ge(tail_done, 1)
            for e in range(NE):
                pool.indirect_dma_start(scratch[0:NE * REGION, :], bass.IndirectOffsetOnAxis(tail_i[:, e:e + 1], 0),
                                        nobody_row[:], None).then_inc(tails_written, 16)

            def tile(jj, k):
                j = 4 * jj + k
                pool.wait_ge(stats3_done, j + 1)
                take_wait()
                pool.tensor_scalar(var3[:], mv3[k % 2][:, 1:2], EPS, None, ALU.add).then_inc(pool_3, 1)
                pool.wait_ge(pool_3, j + 1)
                take_wait()
                pool.tensor_tensor(rstd3[k % 2][:], var3[:], half_neg[:, 0:1], ALU.pow).then_inc(rstd3_done, 1)
                pool.wait_ge(x3_done, j + 1)
                take_wait()
                pool.indirect_dma_start(out_rows, bass.IndirectOffsetOnAxis(tok_i[k][:, 0:1], 0), x3[k][:], None,
                                        bounds_check=B * P - 1, oob_is_err=False).then_inc(out_written[k], 16)

            with pool.Fori(0, NT // 4) as jj:
                for k in range(4):
                    tile(jj, k)

        @block.scalar
        def _(act):
            def step(i, u):
                n = 2 * i + u
                m, r = n - 1, n - 2

                def capped(g):
                    at_least(act, scores_ready, 4 * n + g + 1)
                    nc.scalar.activation(probs[g][:], ps[:, g % 2, :].rearrange("p (h i) -> p h i", h=4), ACT.Tanh,
                                         scale=1.0 / (DH ** 0.5 * SOFTCAP)).then_inc(tanh_done, 1)

                def exped(g):
                    act.wait_ge(tanh_done, 4 * n + g + 1)
                    nc.scalar.activation(probs[g][:], probs[g][:], ACT.Exp, scale=SOFTCAP).then_inc(exp_done, 1)

                if has(n, 0, B - 1):
                    capped(0)
                    capped(1)
                    exped(0)
                    exped(1)
                    at_least(act, y_kept, n + 1)
                    nc.scalar.activation(gate_e[:], gate_z[:], ACT.Exp, scale=-1.0).then_inc(gate_exp_done, 1)
                if has(n, 0, B - 1):
                    capped(2)
                    capped(3)
                    exped(2)
                    exped(3)
                if has(n, 2, B + 1):
                    at_least(act, one_hot_done, r + 1)
                    nc.scalar.activation(r_exp[:], r_low[:], ACT.Exp, accum_out=r_sum[:]).then_inc(r_exp_done, 1)
                for half in range(2):
                    if has(n, 1, B):
                        at_least(act, shifted, 2 * m + half + 1)
                        part = logits[:, 8 * half:8 * half + 8, :]
                        nc.scalar.activation(part, part, ACT.Exp).then_inc(xexp_done, 1)
                    if has(n, -1, B - 2):
                        at_least(act, proj_ready, 6 * (n + 1) + 5 + half)
                        nc.scalar.copy(v1[1 - u][:, 8 * half:8 * half + 8, 0:DH],
                                       ps[:, 6 + half, :].rearrange("p (h d) -> p h d", d=DH)).then_inc(v_kept, 1)
                    if has(n, 1, B):
                        for g in (2 * half, 2 * half + 1):
                            at_least(act, xpT_ready, 4 * m + g + 1)
                            nc.scalar.copy(xprobsT[:, 4 * g:4 * g + 4, :],
                                           ps[0:S2, 2 + g, :].rearrange("p (h i) -> p h i", h=4)).then_inc(xpT_kept, 1)

            act.wait_ge(pool_const, N_POOL_CONST)
            run_steps(act, step)

            def gelu(j, k):
                act.wait_ge(hid_ready, j + 1)
                nc.scalar.activation(hid[k % 2][:], ps[:, 2 + k % 2, :], ACT.Gelu).then_inc(gelu_done, 1)

            def keep_hidT(j, k):
                act.wait_ge(hidT_ready, j + 1)
                nc.scalar.copy(hidT[k % 2][:], ps[:, 4 + k % 2, :].rearrange("p (c i) -> p c i", c=NFC)).then_inc(
                    hidT_kept, 1)

            gelu(0, 0)
            with act.Fori(0, NT // 4 - 1) as jj:
                for k in range(4):
                    keep_hidT(4 * jj + k, k)
                    gelu(4 * jj + k + 1, k + 1)
            for j in range(NT - 4, NT):
                keep_hidT(j, j)
                if j + 1 < NT:
                    gelu(j + 1, j + 1)

        @block.vector
        def _(dve):
            S, X, R = Chain(dve, dve_s, 8), Chain(dve, dve_x, 4), Chain(dve, dve_r, 9)
            T = Chain(dve, dve_t, 10 + 14)

            def step(i, u):
                n = 2 * i + u
                m, r = n - 1, n - 2
                has_s, has_x, has_r, has_p = (has(n, 0, B - 1), has(n, 1, B), has(n, 2, B + 1), has(n, -1, B - 2))
                S.start(n)
                X.start(m)
                R.start(r)

                def keep_qk(j):
                    if has_p:
                        at_least(dve, proj_ready, 6 * (n + 1) + j + 1)
                        bank, dst = (2, 3, 6, 7)[j], (qT, kT)[j // 2][1 - u]
                        dve.tensor_copy(dst[:, 4 * (j % 2):4 * (j % 2) + 4, :],
                                        ps[:, bank, :].rearrange("p (c t) -> p c t", c=4)).then_inc(qk_kept, 1)

                def normalise(half):
                    at_least(dve, av_ready, 2 * n + half + 1)
                    both = ps[:, 0:2, 0:4 * HEAD_W].rearrange("p g (k d) -> p g k d", d=HEAD_W)
                    g = gate[:, 8 * half:8 * half + 8].rearrange("p (k g) -> p g k", g=2)
                    S.link(dve.reciprocal(rsum[:], both[:, :, :, DH]))
                    S.link(dve.tensor_tensor(rgate[:], rsum[:], g, ALU.mult))
                    dst = attn[:, 512 * half:512 * half + 512].rearrange("p (k g d) -> p g k d", g=2, d=DH)
                    dve.tensor_tensor(dst, both[:, :, :, 0:DH],
                                      rgate[:].unsqueeze(3).broadcast_to([P, 2, 4, DH]),
                                      ALU.mult).then_inc(attn_kept, 1)

                keep_qk(0)
                if has(n, 1, B + 1):
                    at_least(dve, rstd_done, n)
                if has_x:
                    dve.tensor_scalar(x1[1 - u][:], y1[:], mv[:, 0, 0:1], rstd[:, 0:1], ALU.subtract,
                                      ALU.mult).then_inc(x1_done, 1)
                if has_r:
                    at_least(dve, scattered[u], 16 * (i - 1))
                    dve.tensor_scalar(row[u][:, 0:P], y2[:], mv[:, 1, 0:1], rstd[:, 1:2], ALU.subtract,
                                      ALU.mult).then_inc(x2_done, 1)
                keep_qk(1)
                if has_x:
                    at_least(dve, x1T_ready, m + 1)
                    dve.tensor_copy(x1T[:], ps[:, 4, 0:P]).then_inc(x1T_kept, 1)
                if has_r:
                    at_least(dve, x2T_ready, r + 1)
                    dve.tensor_copy(x2T[:], ps[:, 5, 0:P]).then_inc(x2T_kept, 1)
                keep_qk(2)
                if has_r:
                    at_least(dve, router_ready, r + 1)
                    lg = ps[:, 5, 0:NE]
                    R.link(dve.tensor_reduce(r_max[:], lg, AX.X, ALU.max))
                    R.link(dve.tensor_scalar(r_low[:], lg, r_max[:, 0:1], None, ALU.subtract))
                    R.link(dve.scalar_tensor_tensor(r_key[:], lg, r_max[:, 0:1], falling[:], ALU.is_equal, ALU.mult))
                    R.link(dve.tensor_reduce(r_first[:], r_key[:], AX.X, ALU.max))
                    dve.tensor_scalar(one_hot[:], falling[:], r_first[:, 0:1], None,
                                      ALU.is_equal).then_inc(one_hot_done, 1)
                if has_x:
                    at_least(dve, qkv1_ready, m + 1)
                    dve.tensor_scalar(q1T[:], ps[:, 7, 0:P], bq_sb[:, 0:1], None, ALU.add)
                    dve.scalar_tensor_tensor(k_exp[:], ps[:, 7, P:P + S2].unsqueeze(1).broadcast_to([P, 4, S2]),
                                             bk_sb[:, 0:1], in_group[:].unsqueeze(2).broadcast_to([P, 4, S2]),
                                             ALU.add, ALU.mult)
                    dve.tensor_tensor(v_diag, ps[0:S2, 7, 2 * P:3 * P].rearrange("p (c h d) -> p c h d", c=4, h=4),
                                      bv_sb[:, :].rearrange("p (c h d) -> p c h d", c=4, h=4),
                                      ALU.add).then_inc(qkv1_kept, 1)
                if has_s:
                    at_least(dve, gate_exp_done, n + 1)
                    S.link(dve.tensor_scalar(gate_1[:], gate_e[:], 1.0, None, ALU.add))
                    S.link(dve.reciprocal(gate[:], gate_1[:]))
                    normalise(0)
                if has_r:
                    at_least(dve, place_ready, r + 1)
                    R.link(dve.tensor_tensor(r_pos[:], ps[:, 5, P:P + NE], one_hot[:], ALU.mult))
                    R.link(dve.tensor_tensor(counted[:], counted[:], one_hot[:], ALU.add))
                    R.link(dve.tensor_reduce(pos_f[:], r_pos[:], AX.X, ALU.add))
                    R.link(dve.tensor_copy(pos_i[u][:], pos_f[:]))
                    R.link(dve.tensor_scalar(row[u][:, TOKEN:TOKEN + 1], row[u][:, TOKEN:TOKEN + 1], 2.0 * P, None,
                                             ALU.add))
                    dve.wait_ge(r_exp_done, r + 1)
                    dve.reciprocal(row[u][:, PROB:PROB + 1], r_sum[:]).then_inc(row_done, 1)
                for half in range(2):
                    if has_x:
                        for g in (2 * half, 2 * half + 1):
                            at_least(dve, xscores_ready, 4 * m + g + 1)
                            dve.scalar_tensor_tensor(logits[:, 4 * g:4 * g + 4, :],
                                                     ps[:, 2 + g, 0:4 * S2].rearrange("p (h k) -> p h k", h=4),
                                                     XD ** -0.5, mask_sb[:].unsqueeze(1).broadcast_to([P, 4, S2]),
                                                     ALU.mult, ALU.add).then_inc(xscores_kept, 1)
                        heads = slice(8 * half, 8 * half + 8)
                        dve.wait_ge(xscores_kept, 4 * m + 2 * half + 2)
                        X.link(dve.tensor_reduce(lmax[:, heads], logits[:, heads, :], AX.X, ALU.max))
                        dve.tensor_tensor(logits[:, heads, :], logits[:, heads, :],
                                          lmax[:, heads].unsqueeze(2).broadcast_to([P, H // 2, S2]),
                                          ALU.subtract).then_inc(shifted, 1)
                    if half == 0:
                        keep_qk(3)
                if has_s:
                    normalise(1)
                    for k in range(2):
                        at_least(dve, attnT_ready, 2 * n + k + 1)
                        dve.tensor_copy(attnT[:, 4 * k:4 * k + 4, :],
                                        ps[:, k, :].rearrange("p (c i) -> p c i", c=4)).then_inc(attnT_kept, 1)
                if has_x:
                    at_least(dve, xav_ready, m + 1)
                    X.link(dve.reciprocal(xrec[:], ps[:, 6, P:2 * P]))
                    dve.tensor_tensor(xattnT[:], ps[:, 6, 0:P], xrec[:], ALU.mult).then_inc(xattnT_kept, 1)
                if has(n, -1, B - 1):
                    at_least(dve, y_ready, n + 2)
                    if has_s:
                        dve.wait_ge(x_loaded[u], 16 * (i + 1))
                        S.link(dve.tensor_tensor(y1[:], ps[:, 2, 0:P], x_sb[u][:], ALU.add))
                    if has_p:
                        dve.tensor_copy(gate_z[:], ps[:, 2, P:P + H]).then_inc(y_kept, 1)
                    else:
                        dve.sem_inc(y_kept, 1)
                if has_s:
                    S.link(dve.bn_stats(bn[:, 0, :], y1[:]))
                    dve.sem_inc(dve_passed, 1)
                    dve.bn_aggr(mv[:, 0, :], bn[:, 0, :]).then_inc(stats_done, 1)
                    S.end()
                if has_x:
                    at_least(dve, y2_ready, m + 1)
                    dve.wait_ge(x1_bo_done, m + 1)
                    dve.tensor_tensor(y2[:], ps[:, 7, 0:P], x1_bo[:], ALU.add).then_inc(y2_kept, 1)
                    dve.wait_ge(y2_kept, m + 1)
                    X.link(dve.bn_stats(bn[:, 1, :], y2[:]))
                    dve.sem_inc(dve_passed, 1)
                    dve.bn_aggr(mv[:, 1, :], bn[:, 1, :]).then_inc(stats_done, 1)
                    X.end()
                if has_r:
                    R.end()

            def split_biases():
                dve.wait_ge(b_loaded, 32)
                for w in range(2):
                    T.link(dve.tensor_copy(b_part[w][0][:], b_in[w][:]))
                    T.link(dve.tensor_tensor(b_rest[w][:], b_in[w][:], b_part[w][0][:], ALU.subtract))
                    T.link(dve.tensor_copy(b_part[w][1][:], b_rest[w][:]))
                    T.link(dve.tensor_tensor(b_rest[w][:], b_rest[w][:], b_part[w][1][:], ALU.subtract))
                    T.link(dve.tensor_copy(b_part[w][2][:], b_rest[w][:]))
                dve.memset(ones_3[:], 1.0).then_inc(b_split, 1)

            v_diag = bass.AP(v_exp[:].tensor, v_exp[:].offset, [list(v_exp[:].ap[0]), [P, 4], [32 + XD, 4], [1, XD]])
            dve.wait_ge(pool_const, N_POOL_CONST)
            dve.tensor_reduce(in_group[:], head_rows[:, :].rearrange("p (g k) -> p k g", g=4), AX.X,
                              ALU.add).then_inc(dve_const, 1)
            dve.wait_ge(other_w, 16 * N_OTHER)
            dve.tensor_scalar(mask_sb[:], mask_sb[:], -1.0e9, None, ALU.mult).then_inc(dve_const, 1)
            dve.wait_ge(dve_const, 2)
            T.start(0)
            run_steps(dve, step, split_biases)

            dve.wait_ge(count_ready, 1)
            T.link(dve.tensor_copy(tail[:], ps[:, 0, 0:NE]))
            T.link(dve.tensor_scalar(tail_i[:], tail[:], part_f[:, 0:1], None, ALU.add))
            T.link(dve.tensor_tensor(n_rows[:], tail[:], region_of[:], ALU.subtract))
            dve.sem_inc(tail_done, 1)
            T.link(dve.tensor_scalar(n_tiles_i[:], n_rows[:], P - 1.0, None, ALU.add))
            T.link(dve.tensor_scalar(n_tiles_i[:], n_tiles_i[:], P.bit_length() - 1, None, ALU.logical_shift_right))
            T.link(dve.tensor_copy(n_tiles[:], n_tiles_i[:]))
            T.link(dve.tensor_tensor_scan(tile_end[:], ones[:, 0:NE], n_tiles[:], 0.0, ALU.mult, ALU.add))

            def over_tiles(t):
                return t[0:1, :].unsqueeze(1).broadcast_to([1, NT + 1, NE])

            T.link(dve.tensor_tensor(past[:], tile_no[:], over_tiles(tile_end), ALU.is_ge))
            T.link(dve.tensor_reduce(t_exp[:], past[:], AX.X, ALU.add))
            T.link(dve.tensor_tensor(past[:], past[:], over_tiles(n_tiles), ALU.mult))
            T.link(dve.tensor_reduce(t_start[:], past[:], AX.X, ALU.add))
            T.link(dve.tensor_tensor(t_row[:], tile_no[:, :, 0], t_start[:], ALU.subtract))
            T.link(dve.tensor_scalar(t_start[:], t_exp[:], float(REGION), None, ALU.mult))
            T.link(dve.scalar_tensor_tensor(t_row[:], t_row[:], float(P), t_start[:], ALU.mult, ALU.add))
            dve.tensor_scalar(row_at[:], t_row[:], float(NE * REGION), None, ALU.min).then_inc(table_done, 1)
            dve.tensor_scalar(exp_at[:], t_exp[:], NE - 1.0, None, ALU.min).then_inc(table_done, 1)
            T.end()

            def keep_xeT(j, k):
                dve.wait_ge(xeT_ready, j + 1)
                dve.tensor_copy(xeT[k % 2][:], ps[:, k % 2, 0:P]).then_inc(xeT_kept, 1)

            def residual(j, k, jj):
                dve.wait_ge(y3_ready, j + 1)
                at_least(dve, x3_done, j - 1)
                dve.scalar_tensor_tensor(y3[k % 2][:], ps[:, 6 + k % 2, 0:P], trow[k][:, PROB:PROB + 1],
                                         trow[k][:, 0:P], ALU.mult, ALU.add).then_inc(y3_kept, 1)
                at_least(dve, out_written[k], 16 * jj)
                dve.tensor_copy(tok_i[k][:], trow[k][:, TOKEN:TOKEN + 1])
                dve.wait_ge(y3_kept, j + 1)
                dve.bn_stats(bn3[:], y3[k % 2][:]).then_inc(dve_3, 1)
                dve.wait_ge(dve_3, j + 1)
                dve.sem_inc(dve_passed, 1)
                dve.bn_aggr(mv3[k % 2][:], bn3[:]).then_inc(stats3_done, 1)

            def norm3(j, k):
                dve.wait_ge(rstd3_done, j + 1)
                dve.tensor_scalar(x3[k][:], y3[k % 2][:], mv3[k % 2][:, 0:1], rstd3[k % 2][:, 0:1], ALU.subtract,
                                  ALU.mult).then_inc(x3_done, 1)

            keep_xeT(0, 0)
            keep_xeT(1, 1)
            for j in range(4):
                keep_xeT(j + 2, j + 2)
                residual(j, j, 0)
                if j:
                    norm3(j - 1, j - 1)
            with dve.Fori(1, NT // 4 - 1) as jj:
                for k in range(4):
                    keep_xeT(4 * jj + k + 2, k + 2)
                    residual(4 * jj + k, k, jj)
                    norm3(4 * jj + k - 1, (k - 1) % 4)
            for k in range(4):
                j = NT - 4 + k
                if j + 2 < NT:
                    keep_xeT(j + 2, k + 2)
                residual(j, k, NT // 4 - 1)
                norm3(j - 1, (k - 1) % 4)
            norm3(NT - 1, 3)

        @block.tensor
        def _(pe):
            mm, tr = pe.matmul, pe.transpose

            def step(i, u):
                n = 2 * i + u
                m, r = n - 1, n - 2
                has_s, has_x, has_r, has_p = (has(n, 0, B - 1), has(n, 1, B), has(n, 2, B + 1), has(n, -1, B - 2))

                def scores(g):
                    if g == 0:
                        at_least(pe, qk_kept, 4 * (n + 1))
                        at_least(pe, attnT_kept, 2 * n)
                    else:
                        at_least(pe, tanh_done, 4 * n + 2)
                    for k in range(4):
                        for w in range(2):
                            h = head_of(g + w, k)
                            rows = slice(DH * (h % 2), DH * (h % 2) + DH)
                            last = mm(ps[:, w, k * P:(k + 1) * P], kT[u][rows, h // 2, :], qT[u][rows, h // 2, :],
                                      start=True, stop=True)
                            if k == 3:
                                last.then_inc(scores_ready, 1)

                def project(j, chunk=None):
                    if not has_p:
                        return
                    bank = (2, 3, 6, 7, 6, 7)[j]
                    xt = xT_sb[1 - u]
                    if j == 0:
                        pe.wait_ge(xT_loaded[1 - u], 16 * (i + u + 1))
                        at_least(pe, y_kept, n + 1)
                    elif j == 1:
                        at_least(pe, xpT_kept, 4 * (n - 2) + 2)
                    elif j == 4:
                        at_least(pe, qk_kept, 4 * (n + 1) + 3)
                    elif j == 5:
                        at_least(pe, qk_kept, 4 * (n + 1) + 4)
                    if j < 4:
                        for c in range(4) if chunk is None else (chunk,):
                            e = (j // 2) * INNER + (4 * (j % 2) + c) * P
                            last = mm(ps[:, bank, c * P:(c + 1) * P], wqkv_sb[:, e:e + P], xt[:], start=True, stop=True)
                    else:
                        e = 2 * INNER + 512 * (j - 4)
                        last = mm(ps[:, bank, :], xt[:], wqkv_sb[:, e:e + 512], start=True, stop=True)
                    if chunk is None or chunk == 3:
                        last.then_inc(proj_ready, 1)

                def weigh(half):
                    if half == 0:
                        at_least(pe, tanh_done, 4 * n + 4)
                        at_least(pe, v_kept, 2 * (n + 1))
                    else:
                        at_least(pe, attn_kept, 2 * n + 1)
                    for w in range(2):
                        g = 2 * half + w
                        at_least(pe, causal_done, 4 * n + g + 1)
                        for k in range(4):
                            last = mm(ps[:, w, k * HEAD_W:(k + 1) * HEAD_W], probs[g][:, k, :],
                                      v1[u][:, head_of(g, k), :], start=True, stop=True)
                    last.then_inc(av_ready, 1)

                def transpose_probs(half):
                    at_least(pe, xexp_done, 2 * m + half + 1)
                    for g in (2 * half, 2 * half + 1):
                        at_least(pe, xscores_kept, 4 * m + g + 1)
                        for k in range(4):
                            last = tr(ps[0:S2, 2 + g, k * P:(k + 1) * P], logits[:, 4 * g + k, :], ident[:])
                        last.then_inc(xpT_ready, 1)

                if has_s:
                    if isinstance(n, int) and n < 2:
                        pe.wait_ge(v_kept, 2 * (n + 1))
                    scores(0)
                project(0)
                project(1)
                if has_s:
                    scores(2)
                if has_x:
                    at_least(pe, xpT_kept, 4 * (n - 2) + 3)
                    at_least(pe, x1_done, m + 1)
                    tr(ps[:, 4, 0:P], x1[1 - u][:], ident[:]).then_inc(x1T_ready, 1)
                if has_r:
                    at_least(pe, xpT_kept, 4 * (n - 1))
                    at_least(pe, x2_done, r + 1)
                    tr(ps[:, 5, 0:P], row[u][:, 0:P], ident[:]).then_inc(x2T_ready, 1)
                project(2)
                if has_r:
                    at_least(pe, x2T_kept, r + 1)
                    mm(ps[:, 5, 0:NE], x2T[:], wr_sb[:], start=True, stop=True).then_inc(router_ready, 1)
                if has_x:
                    at_least(pe, y2_kept, n - 1)
                    at_least(pe, x1T_kept, m + 1)
                    at_least(pe, ctx_loaded[1 - u], 16 * (i + u))
                    mm(ps[:, 7, 0:P], wq_sb[:], x1T[:], start=True, stop=True)
                    mm(ps[:, 7, P:P + S2], wk_sb[:], ctx_sb[1 - u][:], start=True, stop=True)
                    mm(ps[0:S2, 7, 2 * P:3 * P], ctx_sb[1 - u][:], wv_sb[:], start=True,
                       stop=True).then_inc(qkv1_ready, 1)
                if has_s:
                    weigh(0)
                if has_r:
                    at_least(pe, one_hot_done, r + 1)
                    mm(ps[:, 5, P:P + NE], before[:], one_hot[:], start=True, stop=False)
                    mm(ps[:, 5, P:P + NE], ones[:], counted[:], start=False, stop=True).then_inc(place_ready, 1)
                if has_x:
                    at_least(pe, qkv1_kept, m + 1)
                for g in range(4):
                    if has_x:
                        if has_p and g < 2:
                            at_least(pe, qk_kept, 4 * (n + 1) + g + 1)
                        elif g == 0:
                            at_least(pe, y_kept, min(n + 1, B + 1))
                        elif g == 1:
                            at_least(pe, xpT_kept, 4 * (n - 2) + 2)
                        elif g == 3 and has_r:
                            at_least(pe, row_done, r + 1)
                        rows = slice(32 * g, 32 * g + 32)
                        mm(ps[:, 2 + g, 0:4 * S2], q1T[rows, :], k_exp[rows, :, :].rearrange("p h k -> p (h k)"),
                           start=True, stop=True).then_inc(xscores_ready, 1)
                    project(3, g)
                project(4)
                if has_x:
                    transpose_probs(0)
                if has_s:
                    weigh(1)
                project(5)
                if has_x:
                    transpose_probs(1)
                if has_s:
                    at_least(pe, attn_kept, 2 * n + 2)
                    for w in range(2):
                        for c in range(4):
                            last = tr(ps[:, w, c * P:(c + 1) * P], attn[:, (4 * w + c) * P:(4 * w + c + 1) * P],
                                      ident[:])
                        last.then_inc(attnT_ready, 1)
                if has_x:
                    at_least(pe, xpT_kept, 4 * m + 4)
                    if has_p:
                        at_least(pe, v_kept, 2 * (n + 1) + 1)
                    for what, col in ((None, 0), (ones_exp, P)):
                        for k in range(4):
                            for c in range(4):
                                lhsT = v_exp[:, 4 * c + k, :] if what is None else what[:, k, :]
                                last = mm(ps[32 * c:32 * c + 32, 6, col:col + P], lhsT, xprobsT[:, 4 * c + k, :],
                                          start=(k == 0), stop=(k == 3))
                    last.then_inc(xav_ready, 1)
                if has(n, -1, B - 1):
                    if isinstance(n, int) and n < 0:
                        pe.wait_ge(qk_kept, 1)
                    if has_s:
                        for c in range(NCH):
                            at_least(pe, attnT_kept, 2 * n + c // 4 + 1)
                            last = mm(ps[:, 2, 0:P], attnT[:, c, :], wout_sb[:, c, :], start=(c == 0),
                                      stop=(c == NCH - 1))
                    if has_p:
                        last = mm(ps[:, 2, P:P + H], xT_sb[1 - u][:], wg_sb[:], start=True, stop=True)
                    last.then_inc(y_ready, 1)
                if has_x:
                    if has_p:
                        at_least(pe, v_kept, 2 * (n + 1) + 2)
                    at_least(pe, xattnT_kept, m + 1)
                    mm(ps[:, 7, 0:P], xattnT[:], wo_sb[:], start=True, stop=True).then_inc(y2_ready, 1)

            pe.wait_ge(first_w, 16 * N_FIRST)
            pe.wait_ge(pool_const, N_POOL_CONST)
            pe.wait_ge(other_w, 16 * N_OTHER)
            run_steps(pe, step)

            pe.wait_ge(row_done, B)
            mm(ps[:, 0, 0:NE], ones[:], counted[:], start=True, stop=True).then_inc(count_ready, 1)

            def T(j, k, jj):
                pe.wait_ge(trow_loaded[k], 16 * (jj + 1))
                at_least(pe, xeT_kept, j - 1)
                tr(ps[:, k % 2, 0:P], trow[k][:, 0:P], ident[:]).then_inc(xeT_ready, 1)

            def hidden(j, k, e):
                pe.wait_ge(xeT_kept, j + 1)
                at_least(pe, gelu_done, j - 1)
                mm(ps[:, 2 + k % 2, :], ones_3[:], b1_3[:, bass.ds(e * FF, FF)], start=True, stop=False)
                mm(ps[:, 2 + k % 2, :], xeT[k % 2][:], w1_sb[:, bass.ds(e * FF, FF)], start=False,
                   stop=True).then_inc(hid_ready, 1)

            def hidden_T(j, k):
                pe.wait_ge(gelu_done, j + 1)
                at_least(pe, hidT_kept, j - 1)
                for c in range(NFC):
                    last = tr(ps[:, 4 + k % 2, c * P:(c + 1) * P], hid[k % 2][:, c * P:(c + 1) * P], ident[:])
                last.then_inc(hidT_ready, 1)

            def output(j, k, e):
                pe.wait_ge(hidT_kept, j + 1)
                at_least(pe, y3_kept, j - 1)
                mm(ps[:, 6 + k % 2, 0:P], ones_3[:], b2_3[:, bass.ds(e * P, P)], start=True, stop=False)
                for c in range(NFC):
                    last = mm(ps[:, 6 + k % 2, 0:P], hidT[k % 2][:, c, :], w2_sb[:, bass.ds(e * FF + c * P, P)],
                              start=False, stop=(c == NFC - 1))
                last.then_inc(y3_ready, 1)

            def expert(j):
                return pe.value_load(exp_at[0:1, bass.ds(j, 1)], min_val=0, max_val=NE - 1)

            pe.wait_ge(ffn_w, 16 * N_FFN)
            pe.wait_ge(b_placed, 16 * 6)
            pe.wait_ge(table_done, 2)
            T(0, 0, 0)
            T(1, 1, 0)
            hidden(0, 0, expert(0))

            def four(jj, last):
                e = [expert(4 * jj + k) for k in range(4 if last else 5)]
                for k in range(4):
                    j = 4 * jj + k
                    if not last or k < 2:
                        T(j + 2, (k + 2) % 4, jj + (k + 2) // 4)
                    hidden_T(j, k)
                    if not last or k < 3:
                        hidden(j + 1, k + 1, e[k + 1])
                    output(j, k, e[k])

            four(0, False)
            with pe.Fori(1, NT // 4 - 1) as jj:
                four(jj, False)
            four(NT // 4 - 1, True)


_OUT = (B, P, P)


def kernel(x, ctx_1024, mask_1x1xSxS2_fk1, L0_attn_w_qkv, L0_attn_w_gates, L0_attn_w_out,
           L0_xattn_wq, L0_xattn_bq, L0_xattn_wk, L0_xattn_bk, L0_xattn_wv, L0_xattn_bv, L0_xattn_wo, L0_xattn_bo,
           L0_ffn_Wr, L0_ffn_W1, L0_ffn_b1, L0_ffn_W2, L0_ffn_b2):
    import numpy as np
    import concourse.bacc as bacc
    from concourse.bass_utils import run_bass_kernel_spmd

    x = np.asarray(x)
    ctx = np.asarray(ctx_1024)
    arrays = {
        "x": x.reshape(B * P, P),
        "xT": x.transpose(2, 0, 1).reshape(P, B * P),
        "ctxT": ctx.transpose(2, 0, 1).reshape(P, B * S2),
        "mask": np.asarray(mask_1x1xSxS2_fk1).reshape(P, S2),
        "w_qkv": L0_attn_w_qkv, "w_gates": L0_attn_w_gates, "w_out": L0_attn_w_out,
        "wq": L0_xattn_wq, "bq": np.asarray(L0_xattn_bq).reshape(P, 1),
        "wk": L0_xattn_wk, "bk": np.asarray(L0_xattn_bk).reshape(P, 1),
        "wv": L0_xattn_wv, "bv": L0_xattn_bv, "wo": L0_xattn_wo, "bo": L0_xattn_bo,
        "Wr": L0_ffn_Wr, "W1": L0_ffn_W1, "b1": L0_ffn_b1, "W2": L0_ffn_W2, "b2": L0_ffn_b2,
    }
    nc = bacc.Bacc("TRN2", target_bir_lowering=False, num_devices=1)
    args, ins = [], {}
    for name, a in arrays.items():
        a = np.ascontiguousarray(a)
        ins[f"in_{name}"] = a
        args.append(nc.dram_tensor(f"in_{name}", a.shape, mybir.dt.from_np(a.dtype), kind="ExternalInput").ap())
    out = nc.dram_tensor("out", _OUT, F32, kind="ExternalOutput").ap()
    decoder_layer(nc, *args, out)
    r = run_bass_kernel_spmd(nc, [ins], core_ids=[0])
    return r.results[0]["out"]
```

```python
from contextlib import ExitStack

import concourse.bass as bass
from concourse import mybir

ALU = mybir.AluOpType
ACT = mybir.ActivationFunctionType
AX = mybir.AxisListType
F32 = mybir.dt.float32
BF16 = mybir.dt.bfloat16
I32 = mybir.dt.int32

P = 128
B = 32
H, DH = 16, 64
INNER = H * DH
NCH = INNER // P
SOFTCAP = 50.0
S2 = 77
XD = P // H
NE, FF = 8, 512
NFC = FF // P
REGION = B * P + P
NT = 40
ROW = P + 4
PROB, TOKEN = P, P + 1
NOBODY = 8000.0
EPS = 1e-5
HEAD_W = DH + 1


def head_of(wave, k):
    return 8 * (wave // 2) + 2 * k + wave % 2


class Chain:

    def __init__(self, eng, sem, per):
        self.eng, self.sem, self.per = eng, sem, per

    def start(self, batch):
        self.base, self.k = batch * self.per, 0

    def mark(self, ins):
        self.k += 1
        ins.then_inc(self.sem, 1)

    def need(self):
        self.eng.wait_ge(self.sem, self.base + self.k)

    def link(self, ins):
        self.mark(ins)
        self.need()

    def end(self):
        assert self.k == self.per, (self.k, self.per)


def at_least(eng, sem, value):
    if not isinstance(value, int) or value > 0:
        eng.wait_ge(sem, value)


def has(n, low, high):
    return not isinstance(n, int) or low <= n <= high


def run_steps(eng, step, early=lambda: None):
    step(-1, 1)
    step(0, 0)
    step(0, 1)
    early()
    step(1, 0)
    step(1, 1)
    with eng.Fori(2, B // 2 - 1) as i:
        step(i, 0)
        step(i, 1)
    for i in (B // 2 - 1, B // 2):
        step(i, 0)
        step(i, 1)


def decoder_layer(nc, x, xT, ctxT, mask, w_qkv, w_gates, w_out, wq, bq, wk, bk, wv, bv, wo, bo,
                  Wr, W1, b1, W2, b2, out):
    out_rows = out.rearrange("b s d -> (b s) d")
    scratch = nc.dram_tensor("scratch", [NE * REGION + P, ROW], F32, kind="Internal").ap()

    with ExitStack() as ctx:
        def sb(name, shape, dt=F32):
            return ctx.enter_context(nc.sbuf_tensor(name, shape, dt))

        def sem(name):
            return ctx.enter_context(nc.semaphore(name))

        ps = ctx.enter_context(nc.psum_tensor("ps", [P, 8, 512], F32))

        wqkv_sb = sb("wqkv_sb", [P, 3 * INNER])
        wg_sb = sb("wg_sb", [P, H])
        wout_sb = sb("wout_sb", [P, NCH, P])
        wq_sb, wk_sb, wv_sb, wo_sb = (sb(f"{w}_sb", [P, P]) for w in ("wq", "wk", "wv", "wo"))
        bq_sb, bk_sb = sb("bq_sb", [P, 1]), sb("bk_sb", [P, 1])
        bv_sb, bo_sb = sb("bv_sb", [S2, P]), sb("bo_sb", [P, P])
        wr_sb = sb("wr_sb", [P, NE])
        w1_sb = sb("w1_sb", [P, NE * FF])
        w2_sb = sb("w2_sb", [P, NE * NFC * P])
        mask_sb = sb("mask_sb", [P, S2])
        ident = sb("ident", [P, P])
        before = sb("before", [P, P])
        ones = sb("ones", [P, P])
        head_rows = sb("head_rows", [P, H])
        in_group = sb("in_group", [P, 4])
        before_b = sb("before_b", [P, P], BF16)
        ones_b = sb("ones_b", [P, P], BF16)
        falling = sb("falling", [P, NE])
        region_of = sb("region_of", [P, NE])
        half_neg = sb("half_neg", [P, 2])

        xT_sb = [sb(f"xT_sb{u}", [P, P]) for u in range(2)]
        x_sb = [sb(f"x_sb{u}", [P, P]) for u in range(2)]
        ctx_sb = [sb(f"ctx_sb{u}", [P, S2]) for u in range(2)]
        qT = [sb(f"qT{u}", [P, NCH, P]) for u in range(2)]
        kT = [sb(f"kT{u}", [P, NCH, P]) for u in range(2)]
        v1 = [sb(f"v1{u}", [P, H, HEAD_W]) for u in range(2)]
        probs = [sb(f"probs{g}", [P, 4, P]) for g in range(4)]
        gate_z, gate_e, gate_1, gate = (sb(f"gate_{s}", [P, H]) for s in ("z", "e", "1", "g"))
        rsum = sb("rsum", [P, 2, 4])
        rgate = sb("rgate", [P, 2, 4])
        attn = sb("attn", [P, INNER])
        attnT = sb("attnT", [P, NCH, P])
        y1 = sb("y1", [P, P])
        y2 = sb("y2", [P, P])
        bn = sb("bn", [P, 2, 6])
        mv = sb("mv", [P, 2, 2])
        var_eps = sb("var_eps", [P, 2])
        rstd = sb("rstd", [P, 2])
        x1 = [sb(f"x1_{u}", [P, P]) for u in range(2)]
        x1_bo = sb("x1_bo", [P, P])
        x1T = sb("x1T", [P, P])
        q1T = sb("q1T", [P, P])
        k_exp = sb("k_exp", [P, 4, S2])
        v_exp = sb("v_exp", [S2, H, 32])
        logits = sb("logits", [P, H, S2])
        lowest = sb("lowest", [P, H])
        xsum = sb("xsum", [P, H])
        xrec = sb("xrec", [P, H])
        xprobsT = sb("xprobsT", [S2, H, P])
        xattnT = sb("xattnT", [P, P])
        row = [sb(f"row{u}", [P, ROW]) for u in range(2)]
        x2T = sb("x2T", [P, P])
        r_max = sb("r_max", [P, 1])
        r_low = sb("r_low", [P, NE])
        r_exp = sb("r_exp", [P, NE])
        r_sum = sb("r_sum", [P, 1])
        r_key = sb("r_key", [P, NE])
        r_first = sb("r_first", [P, 1])
        one_hot = sb("one_hot", [P, NE])
        one_hot_b = sb("one_hot_b", [P, NE], BF16)
        placed = sb("placed", [P, NE])
        r_at = sb("r_at", [P, NE])
        r_pos = sb("r_pos", [P, NE])
        pos_f = sb("pos_f", [P, 1])
        pos_i = [sb(f"pos_i{u}", [P, 1], I32) for u in range(2)]

        n_rows = sb("n_rows", [P, NE])
        n_tiles_i = sb("n_tiles_i", [P, NE], I32)
        n_tiles = sb("n_tiles", [P, NE])
        tile_end = sb("tile_end", [P, NE])
        part_f = sb("part_f", [P, 1])
        tail_i = sb("tail_i", [P, NE], I32)
        tile_no = sb("tile_no", [1, NT + 1, NE])
        past = sb("past", [1, NT + 1, NE])
        t_exp, t_start, t_row = (sb(f"t_{s}", [1, NT + 1]) for s in ("exp", "start", "row"))
        row_at = sb("row_at", [1, NT + 1], I32)
        exp_at = sb("exp_at", [1, NT + 1], I32)
        nobody_row = sb("nobody_row", [P, ROW])

        b_in = [sb("b1_in", [P, NE * FF // P]), sb("b2_in", [P, NE])]
        b_rest = [sb("b1_rest", [P, NE * FF // P]), sb("b2_rest", [P, NE])]
        b_part = [[sb(f"b{w + 1}_part{k}", [P, n], BF16) for k in range(3)] for w, n in enumerate((NE * FF // P, NE))]
        b1_3 = sb("b1_3", [3, NE * FF], BF16)
        b2_3 = sb("b2_3", [3, NE * P], BF16)
        ones_3 = sb("ones_3", [3, P], BF16)
        trow = [sb(f"trow{k}", [P, ROW]) for k in range(4)]
        xeT = [sb(f"xeT{k}", [P, P]) for k in range(2)]
        hid = [sb(f"hid{k}", [P, FF]) for k in range(2)]
        hidT = [sb(f"hidT{k}", [P, NFC, P]) for k in range(2)]
        y3 = [sb(f"y3_{k}", [P, P]) for k in range(2)]
        bn3 = sb("bn3", [P, 6])
        mv3 = [sb(f"mv3_{k}", [P, 2]) for k in range(2)]
        var3 = sb("var3", [P, 1])
        rstd3 = [sb(f"rstd3_{k}", [P, 1]) for k in range(2)]
        x3 = [sb(f"x3_{k}", [P, P]) for k in range(4)]
        tok_i = [sb(f"tok_i{k}", [P, 1], I32) for k in range(4)]

        first_w, other_w, ffn_w, b_loaded = sem("first_w"), sem("other_w"), sem("ffn_w"), sem("b_loaded")
        xT_loaded = [sem(f"xT_loaded{u}") for u in range(2)]
        x_loaded = [sem(f"x_loaded{u}") for u in range(2)]
        ctx_loaded = [sem(f"ctx_loaded{u}") for u in range(2)]
        pool_const, dve_const = sem("pool_const"), sem("dve_const")
        proj_ready, qk_kept, v_kept = sem("proj_ready"), sem("qk_kept"), sem("v_kept")
        scores_ready, tanh_done, exp_done, causal_done = (
            sem("scores_ready"), sem("tanh_done"), sem("exp_done"), sem("causal_done"))
        av_ready, attn_kept = sem("av_ready"), sem("attn_kept")
        attnT_ready, attnT_kept = sem("attnT_ready"), sem("attnT_kept")
        y_ready, y_kept = sem("y_ready"), sem("y_kept")
        gates_ready, gates_kept, gate_exp_done = sem("gates_ready"), sem("gates_kept"), sem("gate_exp_done")
        stats1_done, stats2_done, rstd_done = sem("stats1_done"), sem("stats2_done"), sem("rstd_done")
        x1_done, x1_bo_done, x2_done = sem("x1_done"), sem("x1_bo_done"), sem("x2_done")
        x1T_ready, x1T_kept = sem("x1T_ready"), sem("x1T_kept")
        qkv1_ready, qkv1_kept = sem("qkv1_ready"), sem("qkv1_kept")
        xscores_ready, xscores_kept = sem("xscores_ready"), sem("xscores_kept")
        lowest_done, shifted, xexp_done = sem("lowest_done"), sem("shifted"), sem("xexp_done")
        xrec_done, xnorm_done = sem("xrec_done"), [sem(f"xnorm_done{k}") for k in range(2)]
        xpT_ready, xpT_kept, xpT3_kept = sem("xpT_ready"), sem("xpT_kept"), sem("xpT3_kept")
        xav_ready, xattnT_kept = sem("xav_ready"), sem("xattnT_kept")
        y2_ready, y2_kept = sem("y2_ready"), sem("y2_kept")
        x2T_ready, x2T_kept = sem("x2T_ready"), sem("x2T_kept")
        router_ready, router_kept, r_exp_done = sem("router_ready"), sem("router_kept"), sem("r_exp_done")
        one_hot_done, place_ready, place_kept = sem("one_hot_done"), sem("place_ready"), sem("place_kept")
        row_done = sem("row_done")
        scattered = [sem(f"scattered{u}") for u in range(2)]
        dve_s, dve_x, dve_r, dve_t = sem("dve_s"), sem("dve_x"), sem("dve_r"), sem("dve_t")
        pool_ln = sem("pool_ln")
        pool_passed, dve_passed = sem("pool_passed"), sem("dve_passed")
        tail_done, tails_written, table_done = sem("tail_done"), sem("tails_written"), sem("table_done")
        b_split, b_placed = sem("b_split"), sem("b_placed")
        trow_loaded = [sem(f"trow_loaded{k}") for k in range(4)]
        xeT_ready, xeT_kept = sem("xeT_ready"), sem("xeT_kept")
        hid_ready, gelu_done = sem("hid_ready"), sem("gelu_done")
        hidT_ready, hidT_kept = sem("hidT_ready"), sem("hidT_kept")
        y3_ready, y3_kept = sem("y3_ready"), sem("y3_kept")
        stats3_done, rstd3_done, x3_done, pool_3, dve_3 = (
            sem("stats3_done"), sem("rstd3_done"), sem("x3_done"), sem("pool_3"), sem("dve_3"))
        out_written = [sem(f"out_written{k}") for k in range(4)]

        N_FIRST, N_OTHER, N_FFN = 3, 10, 2
        N_POOL_CONST = 22
        N_DVE_CONST = 5
        wqkv_v = wqkv_sb[:, :].rearrange("p (s e) -> p s e", s=3)

        block = ctx.enter_context(nc.Block())

        @block.sync
        def _(sp):
            def load_batch(i, u):
                b = 2 * i + u
                if not (isinstance(b, int) and b < 2):
                    at_least(sp, gates_ready, b - 1)
                sp.dma_start(xT_sb[u][:], xT[:, bass.ds(b * P, P)]).then_inc(xT_loaded[u], 16)
                at_least(sp, qkv1_ready, b - 1)
                sp.dma_start(ctx_sb[u][:], ctxT[:, bass.ds(b * S2, S2)]).then_inc(ctx_loaded[u], 16)
                if not (isinstance(b, int) and b < 2):
                    at_least(sp, y_kept, b - 1)
                sp.dma_start(x_sb[u][:], x[bass.ds(b * P, P), :]).then_inc(x_loaded[u], 16)

            sp.dma_start(wqkv_sb[:], w_qkv).then_inc(first_w, 16)
            sp.dma_start(xT_sb[0][:], xT[:, 0:P]).then_inc(xT_loaded[0], 16)
            sp.dma_start(wg_sb[:], w_gates).then_inc(first_w, 16)
            sp.dma_start(wout_sb[:], w_out.rearrange("(c p) d -> p c d", p=P)).then_inc(first_w, 16)
            sp.dma_start(xT_sb[1][:], xT[:, P:2 * P]).then_inc(xT_loaded[1], 16)
            for u in range(2):
                sp.dma_start(ctx_sb[u][:], ctxT[:, u * S2:(u + 1) * S2]).then_inc(ctx_loaded[u], 16)
                sp.dma_start(x_sb[u][:], x[u * P:(u + 1) * P, :]).then_inc(x_loaded[u], 16)
            for dst, src in ((wq_sb, wq), (wk_sb, wk), (wv_sb, wv), (wo_sb, wo), (bq_sb, bq), (bk_sb, bk),
                             (wr_sb, Wr), (mask_sb, mask)):
                sp.dma_start(dst[:], src).then_inc(other_w, 16)
            sp.dma_start(bv_sb[:], bv.partition_broadcast(S2)).then_inc(other_w, 16)
            sp.dma_start(bo_sb[:], bo.partition_broadcast(P)).then_inc(other_w, 16)
            sp.dma_start(b_in[0][:], b1.rearrange("e (q f) -> (e q) f", q=P // NE)).then_inc(b_loaded, 16)
            sp.dma_start(b_in[1][:], b2.rearrange("e (q f) -> (e q) f", q=P // NE)).then_inc(b_loaded, 16)
            sp.dma_start(w1_sb[:, :].rearrange("p (e f) -> p e f", e=NE),
                         W1.rearrange("e d f -> d e f")).then_inc(ffn_w, 16)
            sp.dma_start(w2_sb[:, :].rearrange("p (e c d) -> p e c d", e=NE, c=NFC),
                         W2.rearrange("e (c p) d -> p e c d", p=P)).then_inc(ffn_w, 16)
            with sp.Fori(1, B // 2) as i:
                load_batch(i, 0)
                load_batch(i, 1)

            sp.wait_ge(b_split, 1)
            for w, dst in enumerate((b1_3, b2_3)):
                for k in range(3):
                    sp.dma_start(dst[k:k + 1, :], b_part[w][k][:]).then_inc(b_placed, 16)

            sp.wait_ge(table_done, 2)
            sp.wait_ge(tails_written, 16 * (NE + 1))
            sp.wait_ge(scattered[0], 16 * (B // 2))
            sp.wait_ge(scattered[1], 16 * (B // 2))

            def load_tile(jj, k):
                start = sp.value_load(row_at[0:1, bass.ds(4 * jj + k, 1)], min_val=0, max_val=NE * REGION)
                at_least(sp, stats3_done, 4 * jj + k - 3)
                sp.dma_start(trow[k][:], scratch[bass.ds(start, P), :]).then_inc(trow_loaded[k], 16)

            for k in range(4):
                load_tile(0, k)
            with sp.Fori(1, NT // 4) as jj:
                for k in range(4):
                    load_tile(jj, k)
            for k in range(4):
                sp.wait_ge(out_written[k], 16 * (NT // 4))

        @block.gpsimd
        def _(pool):
            def select(out_ap, in_ap, pattern, op, base=0, cm=0, fill=0.0):
                return pool.affine_select(out=out_ap, in_=in_ap, pattern=pattern, compare_op=op,
                                          fill=fill, base=base, channel_multiplier=cm)

            count = [0]

            def const(ins):
                ins.then_inc(pool_const, 1)
                count[0] += 1

            def settle():
                pool.wait_ge(pool_const, count[0])

            for t in (ones, ident, before, head_rows):
                const(pool.memset(t[:], 1.0))
            const(pool.memset(v_exp[:], 0.0))
            const(pool.memset(half_neg[:], -0.5))
            const(pool.iota(falling[:], [[-1, NE]], base=NE, channel_multiplier=0,
                            allow_small_or_imprecise_dtypes=True))
            const(pool.iota(region_of[:], [[REGION, NE]], base=0, channel_multiplier=0,
                            allow_small_or_imprecise_dtypes=True))
            const(pool.iota(part_f[:], [[0, 1]], base=0, channel_multiplier=1,
                            allow_small_or_imprecise_dtypes=True))
            const(pool.iota(tile_no[:], [[1, NT + 1], [0, NE]], base=0, channel_multiplier=0,
                            allow_small_or_imprecise_dtypes=True))
            const(pool.memset(nobody_row[:], 0.0))
            for u in range(2):
                const(pool.memset(v1[u][:, :, DH:HEAD_W], 1.0))
                const(pool.memset(row[u][:], 0.0))
            settle()
            const(select(ident[:], ident[:], [[-1, P]], ALU.is_equal, cm=1))
            const(select(before[:], before[:], [[1, P]], ALU.is_gt, cm=-1))
            const(select(head_rows[:], head_rows[:], [[-XD, H]], ALU.is_ge, cm=1))
            const(pool.memset(nobody_row[:, TOKEN:TOKEN + 1], NOBODY))
            for u in range(2):
                const(pool.iota(row[u][:, TOKEN:TOKEN + 1], [[0, 1]], base=(u - 2) * P, channel_multiplier=1,
                                allow_small_or_imprecise_dtypes=True))
            settle()
            const(select(head_rows[:], head_rows[:], [[XD, H]], ALU.is_ge, base=XD - 1, cm=-1))
            assert count[0] == N_POOL_CONST
            settle()
            pool.dma_start(scratch[NE * REGION:NE * REGION + P, :], nobody_row[:]).then_inc(tails_written, 16)

            def take_wait():
                pool.sem_inc(pool_passed, 1)

            def step(i, u):
                n = 2 * i + u
                m, r = n - 1, n - 2

                def causal(g):
                    at_least(pool, exp_done, 4 * n + g + 1)
                    take_wait()
                    select(probs[g][:], probs[g][:], [[0, 4], [1, P]], ALU.is_ge, cm=-1).then_inc(causal_done, 1)

                if has(n, 1, B + 1):
                    a, z = (0 if has(n, 1, B) else 1), (2 if has(n, 2, B + 1) else 1)
                    if has(n, 1, B):
                        at_least(pool, stats1_done, m + 1)
                        take_wait()
                    if has(n, 2, B + 1):
                        at_least(pool, stats2_done, r + 1)
                        take_wait()
                    pool.tensor_scalar(var_eps[:, a:z], mv[:, a:z, 1], EPS, None, ALU.add).then_inc(pool_ln, 1)
                    pool.wait_ge(pool_ln, n)
                    take_wait()
                    pool.tensor_tensor(rstd[:, a:z], var_eps[:, a:z], half_neg[:, a:z], ALU.pow).then_inc(rstd_done, 1)
                if has(n, 1, B):
                    at_least(pool, x1_done, m + 1)
                    take_wait()
                    pool.tensor_tensor(x1_bo[:], x1[1 - u][:], bo_sb[:], ALU.add).then_inc(x1_bo_done, 1)
                if has(n, 0, B - 1):
                    causal(0)
                    causal(1)
                    causal(2)
                    causal(3)
                if has(n, 1, B):
                    at_least(pool, xrec_done, 2 * m + 1)
                    take_wait()
                    pool.tensor_tensor(logits[:, 0:H // 2, :], logits[:, 0:H // 2, :],
                                       xrec[:, 0:H // 2].unsqueeze(2).broadcast_to([P, H // 2, S2]),
                                       ALU.mult).then_inc(xnorm_done[0], 1)
                if has(n, 2, B + 1):
                    at_least(pool, row_done, r + 1)
                    take_wait()
                    pool.indirect_dma_start(scratch[0:NE * REGION, :], bass.IndirectOffsetOnAxis(pos_i[u][:, 0:1], 0),
                                            row[u][:], None).then_inc(scattered[u], 16)
            pool.wait_ge(other_w, 16 * N_OTHER)
            run_steps(pool, step)

            pool.wait_ge(tail_done, 1)
            for e in range(NE):
                pool.indirect_dma_start(scratch[0:NE * REGION, :], bass.IndirectOffsetOnAxis(tail_i[:, e:e + 1], 0),
                                        nobody_row[:], None).then_inc(tails_written, 16)

            def tile(jj, k):
                j = 4 * jj + k
                pool.wait_ge(stats3_done, j + 1)
                take_wait()
                pool.tensor_scalar(var3[:], mv3[k % 2][:, 1:2], EPS, None, ALU.add).then_inc(pool_3, 1)
                pool.wait_ge(pool_3, j + 1)
                take_wait()
                pool.tensor_tensor(rstd3[k % 2][:], var3[:], half_neg[:, 0:1], ALU.pow).then_inc(rstd3_done, 1)
                pool.wait_ge(x3_done, j + 1)
                take_wait()
                pool.indirect_dma_start(out_rows, bass.IndirectOffsetOnAxis(tok_i[k][:, 0:1], 0), x3[k][:], None,
                                        bounds_check=B * P - 1, oob_is_err=False).then_inc(out_written[k], 16)

            with pool.Fori(0, NT // 4) as jj:
                for k in range(4):
                    tile(jj, k)

        @block.scalar
        def _(act):
            def step(i, u):
                n = 2 * i + u
                m, r = n - 1, n - 2

                def capped(g):
                    at_least(act, scores_ready, 4 * n + g + 1)
                    nc.scalar.activation(probs[g][:], ps[:, g % 2, :].rearrange("p (h i) -> p h i", h=4), ACT.Tanh,
                                         scale=1.0 / (DH ** 0.5 * SOFTCAP)).then_inc(tanh_done, 1)

                def exped(g):
                    act.wait_ge(tanh_done, 4 * n + g + 1)
                    nc.scalar.activation(probs[g][:], probs[g][:], ACT.Exp, scale=SOFTCAP).then_inc(exp_done, 1)

                if has(n, 0, B - 1):
                    capped(0)
                    capped(1)
                    exped(0)
                    exped(1)
                    at_least(act, gates_kept, n + 1)
                    nc.scalar.activation(gate_e[:], gate_z[:], ACT.Exp, scale=-1.0).then_inc(gate_exp_done, 1)
                if has(n, 0, B - 1):
                    capped(2)
                    capped(3)
                    exped(2)
                    exped(3)
                if has(n, 2, B + 1):
                    at_least(act, one_hot_done, r + 1)
                    nc.scalar.activation(r_exp[:], r_low[:], ACT.Exp, accum_out=r_sum[:]).then_inc(r_exp_done, 1)
                if has(n, 1, B):
                    at_least(act, lowest_done, m + 1)
                    for h in range(H // 2):
                        last = nc.scalar.activation(logits[:, h, :], logits[:, h, :], ACT.Exp,
                                                    bias=lowest[:, h:h + 1], scale=-1.0,
                                                    accum_out=xsum[:, h:h + 1])
                    last.then_inc(xexp_done, 1)
                    at_least(act, shifted, m + 1)
                    nc.scalar.activation(logits[:, H // 2:H, :], logits[:, H // 2:H, :], ACT.Exp,
                                         scale=-1.0).then_inc(xexp_done, 1)
                if has(n, -1, B - 2):
                    for half in range(2):
                        at_least(act, proj_ready, 6 * (n + 1) + 5 + half)
                        nc.scalar.copy(v1[1 - u][:, 8 * half:8 * half + 8, 0:DH],
                                       ps[:, 6 + half, :].rearrange("p (h d) -> p h d", d=DH)).then_inc(v_kept, 1)
                if has(n, 0, B - 1):
                    for k in range(2):
                        at_least(act, attnT_ready, 2 * n + k + 1)
                        nc.scalar.copy(attnT[:, 4 * k:4 * k + 4, :],
                                       ps[:, k, :].rearrange("p (c i) -> p c i", c=4)).then_inc(attnT_kept, 1)
                if has(n, 1, B):
                    for g in range(3):
                        at_least(act, xpT_ready, 4 * m + g + 1)
                        nc.scalar.copy(xprobsT[:, 4 * g:4 * g + 4, :],
                                       ps[0:S2, 2 + g, :].rearrange("p (h i) -> p h i", h=4)).then_inc(xpT_kept, 1)

            act.wait_ge(pool_const, N_POOL_CONST)
            run_steps(act, step)

            def gelu(j, k):
                act.wait_ge(hid_ready, j + 1)
                nc.scalar.activation(hid[k % 2][:], ps[:, 2 + k % 2, :], ACT.Gelu).then_inc(gelu_done, 1)

            def keep_hidT(j, k):
                act.wait_ge(hidT_ready, j + 1)
                nc.scalar.copy(hidT[k % 2][:], ps[:, 4 + k % 2, :].rearrange("p (c i) -> p c i", c=NFC)).then_inc(
                    hidT_kept, 1)

            gelu(0, 0)
            with act.Fori(0, NT // 4 - 1) as jj:
                for k in range(4):
                    keep_hidT(4 * jj + k, k)
                    gelu(4 * jj + k + 1, k + 1)
            for j in range(NT - 4, NT):
                keep_hidT(j, j)
                if j + 1 < NT:
                    gelu(j + 1, j + 1)

        @block.vector
        def _(dve):
            S, X, R = Chain(dve, dve_s, 7), Chain(dve, dve_x, 2), Chain(dve, dve_r, 10)
            T = Chain(dve, dve_t, 10 + 13)

            def step(i, u):
                n = 2 * i + u
                m, r = n - 1, n - 2
                has_s, has_x, has_r, has_p = (has(n, 0, B - 1), has(n, 1, B), has(n, 2, B + 1), has(n, -1, B - 2))
                S.start(n)
                X.start(m)
                R.start(r)

                def keep_qk(j):
                    if has_p:
                        at_least(dve, proj_ready, 6 * (n + 1) + j + 1)
                        bank, dst = (2, 3, 6, 7)[j], (qT, kT)[j // 2][1 - u]
                        dve.tensor_copy(dst[:, 4 * (j % 2):4 * (j % 2) + 4, :],
                                        ps[:, bank, :].rearrange("p (c t) -> p c t", c=4)).then_inc(qk_kept, 1)

                av_out = ps[:, 0:2, 0:4 * HEAD_W].rearrange("p g (k d) -> p g k d", d=HEAD_W)

                def over_sums(half):
                    at_least(dve, av_ready, 2 * n + half + 1)
                    S.mark(dve.reciprocal(rsum[:], av_out[:, :, :, DH]))

                def with_gates(half):
                    g = gate[:, 8 * half:8 * half + 8].rearrange("p (k g) -> p g k", g=2)
                    S.need()
                    S.mark(dve.tensor_tensor(rgate[:], rsum[:], g, ALU.mult))

                def normalise(half):
                    dst = attn[:, 512 * half:512 * half + 512].rearrange("p (k g d) -> p g k d", g=2, d=DH)
                    S.need()
                    dve.tensor_tensor(dst, av_out[:, :, :, 0:DH],
                                      rgate[:].unsqueeze(3).broadcast_to([P, 2, 4, DH]),
                                      ALU.mult).then_inc(attn_kept, 1)

                def masked(g):
                    at_least(dve, xscores_ready, 4 * m + g + 1)
                    dve.scalar_tensor_tensor(logits[:, 4 * g:4 * g + 4, :],
                                             ps[:, 2 + g, 0:4 * S2].rearrange("p (h k) -> p h k", h=4),
                                             -(XD ** -0.5), mask_sb[:].unsqueeze(1).broadcast_to([P, 4, S2]),
                                             ALU.mult, ALU.add).then_inc(xscores_kept, 1)

                def minimum(half):
                    heads = slice(8 * half, 8 * half + 8)
                    dve.wait_ge(xscores_kept, 4 * m + 2 * half + 2)
                    low = dve.tensor_reduce(lowest[:, heads], logits[:, heads, :], AX.X, ALU.min)
                    if half == 0:
                        low.then_inc(lowest_done, 1)
                    else:
                        X.mark(low)

                def shift():
                    heads = slice(H // 2, H)
                    X.need()
                    dve.tensor_tensor(logits[:, heads, :], logits[:, heads, :],
                                      lowest[:, heads].unsqueeze(2).broadcast_to([P, H // 2, S2]),
                                      ALU.subtract).then_inc(shifted, 1)

                def over_xsums(half):
                    heads = slice(8 * half, 8 * half + 8)
                    dve.wait_ge(xexp_done, 2 * m + half + 1)
                    if half == 1:
                        X.mark(dve.tensor_reduce(xsum[:, heads], logits[:, heads, :], AX.X, ALU.add))
                        X.need()
                    dve.reciprocal(xrec[:, heads], xsum[:, heads]).then_inc(xrec_done, 1)
                    if half == 1:
                        dve.wait_ge(xrec_done, 2 * m + 2)
                        dve.tensor_tensor(logits[:, heads, :], logits[:, heads, :],
                                          xrec[:, heads].unsqueeze(2).broadcast_to([P, H // 2, S2]),
                                          ALU.mult).then_inc(xnorm_done[1], 1)

                if has_r:
                    at_least(dve, y2_ready, r + 1)
                    dve.wait_ge(x1_bo_done, r + 1)
                    dve.tensor_tensor(y2[:], ps[:, 7, 0:P], x1_bo[:], ALU.add).then_inc(y2_kept, 1)
                    dve.wait_ge(y2_kept, r + 1)
                    R.link(dve.bn_stats(bn[:, 1, :], y2[:]))
                    dve.sem_inc(dve_passed, 1)
                    dve.bn_aggr(mv[:, 1, :], bn[:, 1, :]).then_inc(stats2_done, 1)
                keep_qk(0)
                if has(n, 1, B + 1):
                    at_least(dve, rstd_done, n)
                if has_x:
                    dve.tensor_scalar(x1[1 - u][:], y1[:], mv[:, 0, 0:1], rstd[:, 0:1], ALU.subtract,
                                      ALU.mult).then_inc(x1_done, 1)
                if has_r:
                    at_least(dve, scattered[u], 16 * (i - 1))
                    dve.tensor_scalar(row[u][:, 0:P], y2[:], mv[:, 1, 0:1], rstd[:, 1:2], ALU.subtract,
                                      ALU.mult).then_inc(x2_done, 1)
                keep_qk(1)
                if has_x:
                    at_least(dve, x1T_ready, m + 1)
                    dve.tensor_copy(x1T[:], ps[:, 4, 0:P]).then_inc(x1T_kept, 1)
                if has_r:
                    at_least(dve, x2T_ready, r + 1)
                    dve.tensor_copy(x2T[:], ps[:, 5, 0:P]).then_inc(x2T_kept, 1)
                keep_qk(2)
                if has_r:
                    at_least(dve, router_ready, r + 1)
                    lg = ps[:, 5, 0:NE]
                    R.mark(dve.tensor_reduce(r_max[:], lg, AX.X, ALU.max))
                if has_s:
                    at_least(dve, gate_exp_done, n + 1)
                    S.mark(dve.tensor_scalar(gate_1[:], gate_e[:], 1.0, None, ALU.add))
                if has_r:
                    R.need()
                    R.mark(dve.tensor_scalar(r_low[:], lg, r_max[:, 0:1], None, ALU.subtract))
                    R.mark(dve.scalar_tensor_tensor(r_key[:], lg, r_max[:, 0:1], falling[:], ALU.is_equal, ALU.mult))
                if has_s:
                    S.need()
                    S.mark(dve.reciprocal(gate[:], gate_1[:]))
                if has_r:
                    R.need()
                    R.mark(dve.tensor_reduce(r_first[:], r_key[:], AX.X, ALU.max))
                if has_x:
                    at_least(dve, qkv1_ready, m + 1)
                    dve.tensor_scalar(q1T[:], ps[:, 7, 0:P], bq_sb[:, 0:1], None, ALU.add)
                    dve.scalar_tensor_tensor(k_exp[:], ps[:, 7, P:P + S2].unsqueeze(1).broadcast_to([P, 4, S2]),
                                             bk_sb[:, 0:1], in_group[:].unsqueeze(2).broadcast_to([P, 4, S2]),
                                             ALU.add, ALU.mult)
                    dve.tensor_tensor(v_diag, ps[0:S2, 7, 2 * P:3 * P].rearrange("p (c h d) -> p c h d", c=4, h=4),
                                      bv_sb[:, :].rearrange("p (c h d) -> p c h d", c=4, h=4),
                                      ALU.add).then_inc(qkv1_kept, 1)
                if has_r:
                    R.need()
                    dve.tensor_scalar(one_hot_b[:], falling[:], r_first[:, 0:1], None, ALU.is_equal)
                    dve.tensor_scalar(one_hot[:], falling[:], r_first[:, 0:1], None,
                                      ALU.is_equal).then_inc(one_hot_done, 1)
                if has_s:
                    over_sums(0)
                    with_gates(0)
                    normalise(0)
                if has_r:
                    at_least(dve, place_ready, r + 1)
                    R.mark(dve.tensor_tensor(r_at[:], ps[:, 5, P:P + NE], placed[:], ALU.add))
                if has_x:
                    masked(0)
                if has_r:
                    R.need()
                    dve.tensor_tensor(placed[:], ps[:, 5, P + NE:P + 2 * NE], placed[:], ALU.add).then_inc(place_kept, 1)
                if has_r:
                    dve.wait_ge(one_hot_done, r + 1)
                    R.mark(dve.tensor_tensor(r_pos[:], r_at[:], one_hot[:], ALU.mult))
                if has_x:
                    masked(1)
                    minimum(0)
                    masked(2)
                keep_qk(3)
                if has_r:
                    R.need()
                    R.mark(dve.tensor_reduce(pos_f[:], r_pos[:], AX.X, ALU.add))
                if has_x:
                    masked(3)
                if has_r:
                    R.need()
                    R.mark(dve.tensor_copy(pos_i[u][:], pos_f[:]))
                if has_x:
                    minimum(1)
                if has_r:
                    R.mark(dve.tensor_scalar(row[u][:, TOKEN:TOKEN + 1], row[u][:, TOKEN:TOKEN + 1], 2.0 * P, None,
                                             ALU.add))
                    dve.wait_ge(r_exp_done, r + 1)
                    R.need()
                    dve.reciprocal(row[u][:, PROB:PROB + 1], r_sum[:]).then_inc(row_done, 1)
                if has_x:
                    shift()
                if has_s:
                    over_sums(1)
                if has_x:
                    over_xsums(0)
                if has_s:
                    with_gates(1)
                    normalise(1)
                if has_x:
                    over_xsums(1)
                    at_least(dve, xpT_ready, 4 * m + 4)
                    dve.tensor_copy(xprobsT[:, 12:16, :],
                                    ps[0:S2, 5, :].rearrange("p (h i) -> p h i", h=4)).then_inc(xpT3_kept, 1)
                    X.end()
                if has_s:
                    at_least(dve, y_ready, n + 1)
                    dve.wait_ge(x_loaded[u], 16 * (i + 1))
                    dve.tensor_tensor(y1[:], ps[:, 0, 0:P], x_sb[u][:], ALU.add).then_inc(y_kept, 1)
                    dve.wait_ge(y_kept, n + 1)
                    S.link(dve.bn_stats(bn[:, 0, :], y1[:]))
                    dve.sem_inc(dve_passed, 1)
                    dve.bn_aggr(mv[:, 0, :], bn[:, 0, :]).then_inc(stats1_done, 1)
                    S.end()
                if has_x:
                    at_least(dve, xav_ready, m + 1)
                    dve.tensor_copy(xattnT[:], ps[:, 6, 0:P]).then_inc(xattnT_kept, 1)
                if has_p:
                    at_least(dve, gates_ready, n + 2)
                    dve.tensor_copy(gate_z[:], ps[:, 3, 0:H]).then_inc(gates_kept, 1)
                if has_r:
                    R.end()

            def split_biases():
                dve.wait_ge(b_loaded, 32)
                for w in range(2):
                    T.link(dve.tensor_copy(b_part[w][0][:], b_in[w][:]))
                    T.link(dve.tensor_tensor(b_rest[w][:], b_in[w][:], b_part[w][0][:], ALU.subtract))
                    T.link(dve.tensor_copy(b_part[w][1][:], b_rest[w][:]))
                    T.link(dve.tensor_tensor(b_rest[w][:], b_rest[w][:], b_part[w][1][:], ALU.subtract))
                    T.link(dve.tensor_copy(b_part[w][2][:], b_rest[w][:]))
                dve.memset(ones_3[:], 1.0).then_inc(b_split, 1)

            v_diag = bass.AP(v_exp[:].tensor, v_exp[:].offset, [list(v_exp[:].ap[0]), [P, 4], [32 + XD, 4], [1, XD]])
            dve.wait_ge(pool_const, N_POOL_CONST)
            dve.tensor_reduce(in_group[:], head_rows[:, :].rearrange("p (g k) -> p k g", g=4), AX.X,
                              ALU.add).then_inc(dve_const, 1)
            dve.wait_ge(other_w, 16 * N_OTHER)
            dve.tensor_scalar(mask_sb[:], mask_sb[:], 1.0e9, None, ALU.mult).then_inc(dve_const, 1)
            dve.tensor_copy(before_b[:], before[:]).then_inc(dve_const, 1)
            dve.tensor_copy(ones_b[:], ones[:]).then_inc(dve_const, 1)
            dve.tensor_copy(placed[:], region_of[:]).then_inc(dve_const, 1)
            dve.wait_ge(dve_const, N_DVE_CONST)
            T.start(0)
            run_steps(dve, step, split_biases)

            dve.wait_ge(place_kept, B)
            T.link(dve.tensor_scalar(tail_i[:], placed[:], part_f[:, 0:1], None, ALU.add))
            T.link(dve.tensor_tensor(n_rows[:], placed[:], region_of[:], ALU.subtract))
            dve.sem_inc(tail_done, 1)
            T.link(dve.tensor_scalar(n_tiles_i[:], n_rows[:], P - 1.0, None, ALU.add))
            T.link(dve.tensor_scalar(n_tiles_i[:], n_tiles_i[:], P.bit_length() - 1, None, ALU.logical_shift_right))
            T.link(dve.tensor_copy(n_tiles[:], n_tiles_i[:]))
            T.link(dve.tensor_tensor_scan(tile_end[:], ones[:, 0:NE], n_tiles[:], 0.0, ALU.mult, ALU.add))

            def over_tiles(t):
                return t[0:1, :].unsqueeze(1).broadcast_to([1, NT + 1, NE])

            T.link(dve.tensor_tensor(past[:], tile_no[:], over_tiles(tile_end), ALU.is_ge))
            T.link(dve.tensor_reduce(t_exp[:], past[:], AX.X, ALU.add))
            T.link(dve.tensor_tensor(past[:], past[:], over_tiles(n_tiles), ALU.mult))
            T.link(dve.tensor_reduce(t_start[:], past[:], AX.X, ALU.add))
            T.link(dve.tensor_tensor(t_row[:], tile_no[:, :, 0], t_start[:], ALU.subtract))
            T.link(dve.tensor_scalar(t_start[:], t_exp[:], float(REGION), None, ALU.mult))
            T.link(dve.scalar_tensor_tensor(t_row[:], t_row[:], float(P), t_start[:], ALU.mult, ALU.add))
            dve.tensor_scalar(row_at[:], t_row[:], float(NE * REGION), None, ALU.min).then_inc(table_done, 1)
            dve.tensor_scalar(exp_at[:], t_exp[:], NE - 1.0, None, ALU.min).then_inc(table_done, 1)
            T.end()

            def keep_xeT(j, k):
                dve.wait_ge(xeT_ready, j + 1)
                dve.tensor_copy(xeT[k % 2][:], ps[:, k % 2, 0:P]).then_inc(xeT_kept, 1)

            def residual(j, k, jj):
                dve.wait_ge(y3_ready, j + 1)
                at_least(dve, x3_done, j - 1)
                dve.scalar_tensor_tensor(y3[k % 2][:], ps[:, 6 + k % 2, 0:P], trow[k][:, PROB:PROB + 1],
                                         trow[k][:, 0:P], ALU.mult, ALU.add).then_inc(y3_kept, 1)
                at_least(dve, out_written[k], 16 * jj)
                dve.tensor_copy(tok_i[k][:], trow[k][:, TOKEN:TOKEN + 1])
                dve.wait_ge(y3_kept, j + 1)
                dve.bn_stats(bn3[:], y3[k % 2][:]).then_inc(dve_3, 1)
                dve.wait_ge(dve_3, j + 1)
                dve.sem_inc(dve_passed, 1)
                dve.bn_aggr(mv3[k % 2][:], bn3[:]).then_inc(stats3_done, 1)

            def norm3(j, k):
                dve.wait_ge(rstd3_done, j + 1)
                dve.tensor_scalar(x3[k][:], y3[k % 2][:], mv3[k % 2][:, 0:1], rstd3[k % 2][:, 0:1], ALU.subtract,
                                  ALU.mult).then_inc(x3_done, 1)

            keep_xeT(0, 0)
            keep_xeT(1, 1)
            for j in range(4):
                keep_xeT(j + 2, j + 2)
                residual(j, j, 0)
                if j:
                    norm3(j - 1, j - 1)
            with dve.Fori(1, NT // 4 - 1) as jj:
                for k in range(4):
                    keep_xeT(4 * jj + k + 2, k + 2)
                    residual(4 * jj + k, k, jj)
                    norm3(4 * jj + k - 1, (k - 1) % 4)
            for k in range(4):
                j = NT - 4 + k
                if j + 2 < NT:
                    keep_xeT(j + 2, k + 2)
                residual(j, k, NT // 4 - 1)
                norm3(j - 1, (k - 1) % 4)
            norm3(NT - 1, 3)

        @block.tensor
        def _(pe):
            mm, tr = pe.matmul, pe.transpose

            def step(i, u):
                n = 2 * i + u
                m, r = n - 1, n - 2
                has_s, has_x, has_r, has_p = (has(n, 0, B - 1), has(n, 1, B), has(n, 2, B + 1), has(n, -1, B - 2))

                def scores(g):
                    if g == 0:
                        at_least(pe, qk_kept, 4 * (n + 1))
                        at_least(pe, attnT_kept, 2 * n)
                        at_least(pe, y_kept, n)
                    else:
                        at_least(pe, tanh_done, 4 * n + 2)
                    for k in range(4):
                        for w in range(2):
                            h = head_of(g + w, k)
                            rows = slice(DH * (h % 2), DH * (h % 2) + DH)
                            last = mm(ps[:, w, k * P:(k + 1) * P], kT[u][rows, h // 2, :], qT[u][rows, h // 2, :],
                                      start=True, stop=True)
                            if k == 3:
                                last.then_inc(scores_ready, 1)

                def project(j, chunk=None):
                    if not has_p:
                        return
                    bank = (2, 3, 6, 7, 6, 7)[j]
                    xt = xT_sb[1 - u]
                    if j == 0:
                        pe.wait_ge(xT_loaded[1 - u], 16 * (i + u + 1))
                        at_least(pe, xpT_kept, 3 * (n - 2) + 1)
                    elif j == 1:
                        at_least(pe, gates_kept, n + 1)
                        at_least(pe, xpT_kept, 3 * (n - 2) + 2)
                    elif j == 4:
                        at_least(pe, qk_kept, 4 * (n + 1) + 3)
                    elif j == 5:
                        at_least(pe, qk_kept, 4 * (n + 1) + 4)
                    if j < 4:
                        for c in range(4) if chunk is None else (chunk,):
                            e = (j // 2) * INNER + (4 * (j % 2) + c) * P
                            last = mm(ps[:, bank, c * P:(c + 1) * P], wqkv_sb[:, e:e + P], xt[:], start=True, stop=True)
                    else:
                        e = 2 * INNER + 512 * (j - 4)
                        last = mm(ps[:, bank, :], xt[:], wqkv_sb[:, e:e + 512], start=True, stop=True)
                    if chunk is None or chunk == 3:
                        last.then_inc(proj_ready, 1)

                def weigh(half):
                    if half == 0:
                        at_least(pe, tanh_done, 4 * n + 4)
                        at_least(pe, v_kept, 2 * (n + 1))
                    else:
                        at_least(pe, attn_kept, 2 * n + 1)
                    for w in range(2):
                        g = 2 * half + w
                        at_least(pe, causal_done, 4 * n + g + 1)
                        for k in range(4):
                            last = mm(ps[:, w, k * HEAD_W:(k + 1) * HEAD_W], probs[g][:, k, :],
                                      v1[u][:, head_of(g, k), :], start=True, stop=True)
                    last.then_inc(av_ready, 1)

                def project_out(half):
                    at_least(pe, attnT_kept, 2 * n + half + 1)
                    for c in range(4 * half, 4 * half + 4):
                        last = mm(ps[:, 0, 0:P], attnT[:, c, :], wout_sb[:, c, :], start=(c == 0),
                                  stop=(c == NCH - 1))
                    if half:
                        last.then_inc(y_ready, 1)

                def transpose_probs(half):
                    at_least(pe, xnorm_done[half], m + 1)
                    for g in (2 * half, 2 * half + 1):
                        at_least(pe, xscores_kept, 4 * m + g + 1)
                        for k in range(4):
                            last = tr(ps[0:S2, 2 + g, k * P:(k + 1) * P], logits[:, 4 * g + k, :], ident[:])
                        last.then_inc(xpT_ready, 1)

                if has_s:
                    if isinstance(n, int) and n < 2:
                        pe.wait_ge(v_kept, 2 * (n + 1))
                    scores(0)
                if has_r:
                    at_least(pe, v_kept, 2 * min(n + 1, B))
                    at_least(pe, xattnT_kept, r + 1)
                    mm(ps[:, 7, 0:P], xattnT[:], wo_sb[:], start=True, stop=True).then_inc(y2_ready, 1)
                project(0)
                project(1)
                if has_s:
                    scores(2)
                if has_x:
                    at_least(pe, xpT_kept, 3 * (n - 2) + 3)
                    at_least(pe, x1_done, m + 1)
                    tr(ps[:, 4, 0:P], x1[1 - u][:], ident[:]).then_inc(x1T_ready, 1)
                if has_r:
                    at_least(pe, xpT3_kept, n - 1)
                    at_least(pe, x2_done, r + 1)
                    tr(ps[:, 5, 0:P], row[u][:, 0:P], ident[:]).then_inc(x2T_ready, 1)
                project(2)
                if has_r:
                    at_least(pe, x2T_kept, r + 1)
                    mm(ps[:, 5, 0:NE], x2T[:], wr_sb[:], start=True, stop=True).then_inc(router_ready, 1)
                if has_x:
                    at_least(pe, y2_kept, n - 1)
                    at_least(pe, x1T_kept, m + 1)
                    at_least(pe, ctx_loaded[1 - u], 16 * (i + u))
                    mm(ps[:, 7, 0:P], wq_sb[:], x1T[:], start=True, stop=True)
                    mm(ps[:, 7, P:P + S2], wk_sb[:], ctx_sb[1 - u][:], start=True, stop=True)
                    mm(ps[0:S2, 7, 2 * P:3 * P], ctx_sb[1 - u][:], wv_sb[:], start=True,
                       stop=True).then_inc(qkv1_ready, 1)
                if has_s:
                    weigh(0)
                if has_x:
                    at_least(pe, qkv1_kept, m + 1)
                for g in range(4):
                    if has_x:
                        if has_p and g < 2:
                            at_least(pe, qk_kept, 4 * (n + 1) + g + 1)
                        elif g == 0:
                            at_least(pe, xpT_kept, 3 * (n - 2) + 1)
                        elif g == 1:
                            at_least(pe, xpT_kept, 3 * (n - 2) + 2)
                            at_least(pe, gates_kept, B)
                        elif g == 3 and has_r:
                            at_least(pe, place_kept, r + 1)
                        rows = slice(32 * g, 32 * g + 32)
                        mm(ps[:, 2 + g, 0:4 * S2], q1T[rows, :], k_exp[rows, :, :].rearrange("p h k -> p (h k)"),
                           start=True, stop=True).then_inc(xscores_ready, 1)
                    project(3, g)
                    if has_r and g == 0:
                        at_least(pe, one_hot_done, r + 1)
                        mm(ps[:, 5, P:P + NE], before_b[:], one_hot_b[:], start=True, stop=True)
                        mm(ps[:, 5, P + NE:P + 2 * NE], ones_b[:], one_hot_b[:], start=True,
                           stop=True).then_inc(place_ready, 1)
                project(4)
                if has_s:
                    weigh(1)
                project(5)
                if has_s:
                    at_least(pe, attn_kept, 2 * n + 2)
                    for w in range(2):
                        for c in range(4):
                            last = tr(ps[:, w, c * P:(c + 1) * P], attn[:, (4 * w + c) * P:(4 * w + c + 1) * P],
                                      ident[:])
                        last.then_inc(attnT_ready, 1)
                if has_x:
                    transpose_probs(0)
                    transpose_probs(1)
                if has_s:
                    project_out(0)
                    project_out(1)
                if has_x:
                    at_least(pe, xpT_kept, 3 * (m + 1))
                    at_least(pe, xpT3_kept, m + 1)
                    if has_p:
                        at_least(pe, v_kept, 2 * (n + 1) + 1)
                    for k in range(4):
                        for c in range(4):
                            last = mm(ps[32 * c:32 * c + 32, 6, 0:P], v_exp[:, 4 * c + k, :],
                                      xprobsT[:, 4 * c + k, :], start=(k == 0), stop=(k == 3))
                    last.then_inc(xav_ready, 1)
                if has_p:
                    if not has_x:
                        at_least(pe, qk_kept, 4 * (n + 1) + 2)
                    mm(ps[:, 3, 0:H], xT_sb[1 - u][:], wg_sb[:], start=True, stop=True).then_inc(gates_ready, 1)

            pe.wait_ge(first_w, 16 * N_FIRST)
            pe.wait_ge(pool_const, N_POOL_CONST)
            pe.wait_ge(dve_const, N_DVE_CONST)
            pe.wait_ge(other_w, 16 * N_OTHER)
            run_steps(pe, step)

            def T(j, k, jj):
                pe.wait_ge(trow_loaded[k], 16 * (jj + 1))
                at_least(pe, xeT_kept, j - 1)
                tr(ps[:, k % 2, 0:P], trow[k][:, 0:P], ident[:]).then_inc(xeT_ready, 1)

            def hidden(j, k, e):
                pe.wait_ge(xeT_kept, j + 1)
                at_least(pe, gelu_done, j - 1)
                mm(ps[:, 2 + k % 2, :], ones_3[:], b1_3[:, bass.ds(e * FF, FF)], start=True, stop=False)
                mm(ps[:, 2 + k % 2, :], xeT[k % 2][:], w1_sb[:, bass.ds(e * FF, FF)], start=False,
                   stop=True).then_inc(hid_ready, 1)

            def hidden_T(j, k):
                pe.wait_ge(gelu_done, j + 1)
                at_least(pe, hidT_kept, j - 1)
                for c in range(NFC):
                    last = tr(ps[:, 4 + k % 2, c * P:(c + 1) * P], hid[k % 2][:, c * P:(c + 1) * P], ident[:])
                last.then_inc(hidT_ready, 1)

            def output(j, k, e):
                pe.wait_ge(hidT_kept, j + 1)
                at_least(pe, y3_kept, j - 1)
                mm(ps[:, 6 + k % 2, 0:P], ones_3[:], b2_3[:, bass.ds(e * P, P)], start=True, stop=False)
                for c in range(NFC):
                    last = mm(ps[:, 6 + k % 2, 0:P], hidT[k % 2][:, c, :], w2_sb[:, bass.ds(e * FF + c * P, P)],
                              start=False, stop=(c == NFC - 1))
                last.then_inc(y3_ready, 1)

            def expert(j):
                return pe.value_load(exp_at[0:1, bass.ds(j, 1)], min_val=0, max_val=NE - 1)

            pe.wait_ge(ffn_w, 16 * N_FFN)
            pe.wait_ge(b_placed, 16 * 6)
            pe.wait_ge(table_done, 2)
            T(0, 0, 0)
            T(1, 1, 0)
            hidden(0, 0, expert(0))

            def four(jj, last):
                e = [expert(4 * jj + k) for k in range(4 if last else 5)]
                for k in range(4):
                    j = 4 * jj + k
                    if not last or k < 2:
                        T(j + 2, (k + 2) % 4, jj + (k + 2) // 4)
                    hidden_T(j, k)
                    if not last or k < 3:
                        hidden(j + 1, k + 1, e[k + 1])
                    output(j, k, e[k])

            four(0, False)
            with pe.Fori(1, NT // 4 - 1) as jj:
                four(jj, False)
            four(NT // 4 - 1, True)


_OUT = (B, P, P)


def kernel(x, ctx_1024, mask_1x1xSxS2_fk1, L0_attn_w_qkv, L0_attn_w_gates, L0_attn_w_out,
           L0_xattn_wq, L0_xattn_bq, L0_xattn_wk, L0_xattn_bk, L0_xattn_wv, L0_xattn_bv, L0_xattn_wo, L0_xattn_bo,
           L0_ffn_Wr, L0_ffn_W1, L0_ffn_b1, L0_ffn_W2, L0_ffn_b2):
    import numpy as np
    import concourse.bacc as bacc
    from concourse.bass_utils import run_bass_kernel_spmd

    x = np.asarray(x)
    ctx = np.asarray(ctx_1024)
    arrays = {
        "x": x.reshape(B * P, P),
        "xT": x.transpose(2, 0, 1).reshape(P, B * P),
        "ctxT": ctx.transpose(2, 0, 1).reshape(P, B * S2),
        "mask": np.asarray(mask_1x1xSxS2_fk1).reshape(P, S2),
        "w_qkv": L0_attn_w_qkv, "w_gates": L0_attn_w_gates, "w_out": L0_attn_w_out,
        "wq": L0_xattn_wq, "bq": np.asarray(L0_xattn_bq).reshape(P, 1),
        "wk": L0_xattn_wk, "bk": np.asarray(L0_xattn_bk).reshape(P, 1),
        "wv": L0_xattn_wv, "bv": L0_xattn_bv, "wo": L0_xattn_wo, "bo": L0_xattn_bo,
        "Wr": L0_ffn_Wr, "W1": L0_ffn_W1, "b1": L0_ffn_b1, "W2": L0_ffn_W2, "b2": L0_ffn_b2,
    }
    nc = bacc.Bacc("TRN2", target_bir_lowering=False, num_devices=1)
    args, ins = [], {}
    for name, a in arrays.items():
        a = np.ascontiguousarray(a)
        ins[f"in_{name}"] = a
        args.append(nc.dram_tensor(f"in_{name}", a.shape, mybir.dt.from_np(a.dtype), kind="ExternalInput").ap())
    out = nc.dram_tensor("out", _OUT, F32, kind="ExternalOutput").ap()
    decoder_layer(nc, *args, out)
    r = run_bass_kernel_spmd(nc, [ins], core_ids=[0])
    return r.results[0]["out"]
```

```python
from contextlib import ExitStack

import concourse.bass as bass
from concourse import mybir

ALU = mybir.AluOpType
ACT = mybir.ActivationFunctionType
AX = mybir.AxisListType
F32 = mybir.dt.float32
F32R = mybir.dt.float32r
BF16 = mybir.dt.bfloat16
I32 = mybir.dt.int32

P = 128
B = 32
H, DH = 16, 64
INNER = H * DH
NCH = INNER // P
SOFTCAP = 50.0
S2 = 77
XD = P // H
NE, FF = 8, 512
NFC = FF // P
REGION = B * P + P
NT = 40
NBUF = 8
AHEAD = 3
ROW = P + 4
PROB, TOKEN = P, P + 1
NOBODY = 8000.0
EPS = 1e-5
HEAD_W = DH + 1


def head_of(wave, k):
    return 8 * (wave // 2) + 2 * k + wave % 2


class Chain:

    def __init__(self, eng, sem, per):
        self.eng, self.sem, self.per = eng, sem, per

    def start(self, batch):
        self.base, self.k = batch * self.per, 0

    def mark(self, ins):
        self.k += 1
        ins.then_inc(self.sem, 1)

    def need(self):
        self.eng.wait_ge(self.sem, self.base + self.k)

    def link(self, ins):
        self.mark(ins)
        self.need()

    def end(self):
        assert self.k == self.per, (self.k, self.per)


def at_least(eng, sem, value):
    if not isinstance(value, int) or value > 0:
        eng.wait_ge(sem, value)


def has(n, low, high):
    return not isinstance(n, int) or low <= n <= high


def run_steps(eng, step, constants=lambda: None, early=lambda: None):
    step(-1, 2)
    step(-1, 3)
    constants()
    for v in range(4):
        step(0, v)
    early()
    with eng.Fori(1, B // 4 - 1) as q:
        for v in range(4):
            step(q, v)
    for v in range(4):
        step(B // 4 - 1, v)
    step(B // 4, 0)
    step(B // 4, 1)


def decoder_layer(nc, x, xT, ctxT, mask, w_qkv, w_gates, w_out, wq, bq, wk, bk, wv, bv, wo, bo,
                  Wr, W1, b1, W2, b2, out):
    out_rows = out.rearrange("b s d -> (b s) d")
    scratch = nc.dram_tensor("scratch", [NE * REGION + P, ROW], F32, kind="Internal").ap()

    with ExitStack() as ctx:
        def sb(name, shape, dt=F32):
            return ctx.enter_context(nc.sbuf_tensor(name, shape, dt))

        def sem(name):
            return ctx.enter_context(nc.semaphore(name))

        ps = ctx.enter_context(nc.psum_tensor("ps", [P, 8, 512], F32))

        wqkv_sb = sb("wqkv_sb", [P, NE * FF])
        w_hi, w_lo = sb("w_hi", [P, 3 * INNER], F32R), sb("w_lo", [P, 3 * INNER], F32R)
        wg_sb = sb("wg_sb", [P, H])
        wout_sb = sb("wout_sb", [P, NCH, P])
        wq_sb, wk_sb, wv_sb, wo_sb = (sb(f"{w}_sb", [P, P]) for w in ("wq", "wk", "wv", "wo"))
        bq_sb, bk_sb = sb("bq_sb", [P, 1]), sb("bk_sb", [P, 1])
        bv_sb, bo_sb = sb("bv_sb", [S2, P]), sb("bo_sb", [P, P])
        wr_sb = sb("wr_sb", [P, NE])
        w1_sb = sb("w1_sb", [P, NE * FF])
        w2_sb = sb("w2_sb", [P, NFC, NE * P])
        mask_sb = sb("mask_sb", [P, S2])
        ident = sb("ident", [P, P])
        before = sb("before", [P, P])
        ones = sb("ones", [P, P])
        head_rows = sb("head_rows", [P, H])
        in_group = sb("in_group", [P, 4])
        before_b = sb("before_b", [P, P], BF16)
        ones_b = sb("ones_b", [P, P], BF16)
        falling = sb("falling", [P, NE])
        region_of = sb("region_of", [P, NE])
        half_neg = sb("half_neg", [P, 1])

        xT_sb, x_hi, x_lo = ([sb(f"{t}{k}", [P, 2 * P], dt) for k in range(2)]
                             for t, dt in (("xT_sb", F32), ("x_hi", F32R), ("x_lo", F32R)))
        x_sb = [sb(f"x_sb{u}", [P, P]) for u in range(2)]
        ctx_sb = [sb(f"ctx_sb{u}", [P, S2]) for u in range(2)]
        qT = [sb(f"qT{k}", [P, NCH, 2 * P]) for k in range(2)]
        kT = [sb(f"kT{k}", [P, NCH, 2 * P]) for k in range(2)]
        v1 = [sb(f"v1{u}", [P, H, HEAD_W]) for u in range(2)]
        probs = [sb(f"probs{g}", [P, 4, P]) for g in range(4)]
        gate_z, gate_e, gate_1, gate = (sb(f"gate_{s}", [P, H]) for s in ("z", "e", "1", "g"))
        rsum = sb("rsum", [P, 2, 4])
        rgate = sb("rgate", [P, 2, 4])
        attn = sb("attn", [P, INNER])
        attnT = sb("attnT", [P, NCH, P])
        y1 = sb("y1", [P, P])
        y2 = sb("y2", [P, P])
        bn = sb("bn", [P, 2, 6])
        mv = sb("mv", [P, 2, 2])
        var_eps = sb("var_eps", [P, 2])
        rstd = sb("rstd", [P, 2])
        x1 = [sb(f"x1_{u}", [P, P]) for u in range(2)]
        x1_bo = [sb(f"x1_bo{u}", [P, P]) for u in range(2)]
        x1T = sb("x1T", [P, P])
        q1T = sb("q1T", [P, P])
        k_exp = sb("k_exp", [P, 4, S2])
        v_exp = sb("v_exp", [S2, H, 32])
        logits = sb("logits", [P, H, S2])
        lowest = sb("lowest", [P, H])
        xsum = sb("xsum", [P, H])
        xrec = sb("xrec", [P, H])
        xprobsT = sb("xprobsT", [S2, H, P])
        xattnT = sb("xattnT", [P, P])
        row = [sb(f"row{u}", [P, ROW]) for u in range(2)]
        x2T = sb("x2T", [P, P])
        r_max = sb("r_max", [P, 1])
        r_low = sb("r_low", [P, NE])
        r_exp = sb("r_exp", [P, NE])
        r_sum = sb("r_sum", [P, 1])
        r_key = sb("r_key", [P, NE])
        r_first = sb("r_first", [P, 1])
        one_hot = sb("one_hot", [P, NE])
        one_hot_b = sb("one_hot_b", [P, NE], BF16)
        placed = sb("placed", [P, NE])
        r_at = sb("r_at", [P, NE])
        r_pos = sb("r_pos", [P, NE])
        pos_f = sb("pos_f", [P, 1])
        pos_i = [sb(f"pos_i{u}", [P, 1], I32) for u in range(2)]

        n_rows = sb("n_rows", [P, NE])
        n_tiles_i = sb("n_tiles_i", [P, NE], I32)
        n_tiles = sb("n_tiles", [P, NE])
        tile_end = sb("tile_end", [P, NE])
        tail_i = sb("tail_i", [P, NE], I32)
        tile_no = sb("tile_no", [1, NT + 1, NE])
        jump = sb("jump", [P, NE])
        past = sb("past", [1, NT + 1, NE])
        jumps = sb("jumps", [1, NT + 1, NE])
        t_exp, t_jump, t_row = (sb(f"t_{s}", [1, NT + 1]) for s in ("exp", "jump", "row"))
        row_at = sb("row_at", [1, NT + 1], I32)
        exp_at = sb("exp_at", [1, NT + 1], I32)
        nobody_row = sb("nobody_row", [P, 2, ROW])

        b_in = [sb("b1_in", [P, NE * FF // P]), sb("b2_in", [P, NE])]
        b_rest = [sb("b1_rest", [P, NE * FF // P]), sb("b2_rest", [P, NE])]
        b_part = [[sb(f"b{w + 1}_part{k}", [P, n], BF16) for k in range(3)] for w, n in enumerate((NE * FF // P, NE))]
        b1_3 = sb("b1_3", [3, NE * FF], BF16)
        b2_3 = sb("b2_3", [3, NE * P], BF16)
        ones_3 = sb("ones_3", [3, P], BF16)
        trow = [sb(f"trow{k}", [P, ROW]) for k in range(NBUF)]
        xe_hi, xe_lo = ([sb(f"{t}{k}", [P, P], F32R) for k in range(2)] for t in ("xe_hi", "xe_lo"))
        hid = [sb(f"hid{k}", [P, FF]) for k in range(2)]
        hidT = [sb(f"hidT{k}", [P, NFC, P]) for k in range(2)]
        y3 = [sb(f"y3_{k}", [P, P]) for k in range(2)]
        bn3 = sb("bn3", [P, 6])
        mv3 = [sb(f"mv3_{k}", [P, 2]) for k in range(2)]
        var3 = sb("var3", [P, 1])
        rstd3 = [sb(f"rstd3_{k}", [P, 1]) for k in range(2)]
        x3 = [sb(f"x3_{k}", [P, P]) for k in range(4)]
        tok_i = [sb(f"tok_i{k}", [P, 1], I32) for k in range(4)]

        first_w, other_w, ffn_w, b_loaded = sem("first_w"), sem("other_w"), sem("ffn_w"), sem("b_loaded")
        xT_loaded = [sem(f"xT_loaded{u}") for u in range(2)]
        x_loaded = [sem(f"x_loaded{u}") for u in range(2)]
        ctx_loaded = [sem(f"ctx_loaded{u}") for u in range(2)]
        pool_const, dve_const = sem("pool_const"), sem("dve_const")
        w_loaded = [sem(f"w_loaded{k}") for k in range(3)]
        w_hi_done, w_lo_done, x_hi_done, x_lo_done = (
            sem("w_hi_done"), sem("w_lo_done"), sem("x_hi_done"), sem("x_lo_done"))
        qk_ready, v_ready, qk_kept, v_kept = sem("qk_ready"), sem("v_ready"), sem("qk_kept"), sem("v_kept")
        scores_ready, tanh_done, exp_done, causal_done = (
            sem("scores_ready"), sem("tanh_done"), sem("exp_done"), sem("causal_done"))
        av_ready, attn_kept = sem("av_ready"), sem("attn_kept")
        attnT_ready, attnT_kept = sem("attnT_ready"), sem("attnT_kept")
        y_ready, y_kept = sem("y_ready"), sem("y_kept")
        gates_ready, gates_kept, gate_exp_done = sem("gates_ready"), sem("gates_kept"), sem("gate_exp_done")
        stats_done = [sem(f"stats{k}_done") for k in (1, 2)]
        rstd_done = [sem(f"rstd{k}_done") for k in (1, 2)]
        x1_done, x1_bo_done, x2_done = sem("x1_done"), sem("x1_bo_done"), sem("x2_done")
        x1T_ready, x1T_kept = sem("x1T_ready"), sem("x1T_kept")
        qkv1_ready, qkv1_kept = sem("qkv1_ready"), sem("qkv1_kept")
        xscores_ready, xscores_kept = sem("xscores_ready"), sem("xscores_kept")
        lowest_done, shifted, xexp_done = sem("lowest_done"), sem("shifted"), sem("xexp_done")
        xrec_done, xnorm_done = sem("xrec_done"), [sem(f"xnorm_done{k}") for k in range(2)]
        xpT_ready, xpT_kept, xpT_b_kept = sem("xpT_ready"), sem("xpT_kept"), sem("xpT_b_kept")
        xav_ready, xattnT_kept = sem("xav_ready"), sem("xattnT_kept")
        y2_ready, y2_kept = sem("y2_ready"), sem("y2_kept")
        x2T_ready, x2T_kept = sem("x2T_ready"), sem("x2T_kept")
        router_ready, router_kept, r_exp_done = sem("router_ready"), sem("router_kept"), sem("r_exp_done")
        one_hot_done, place_ready, place_kept = sem("one_hot_done"), sem("place_ready"), sem("place_kept")
        row_done = sem("row_done")
        scattered = [sem(f"scattered{u}") for u in range(2)]
        dve_s, dve_x, dve_r, dve_t = sem("dve_s"), sem("dve_x"), sem("dve_r"), sem("dve_t")
        pool_ln = [sem(f"pool_ln{k}") for k in (1, 2)]
        pool_passed, dve_passed = sem("pool_passed"), sem("dve_passed")
        tail_done, tails_written, table_done = sem("tail_done"), sem("tails_written"), sem("table_done")
        b_split, b_placed = sem("b_split"), sem("b_placed")
        trow_loaded = [sem(f"trow_loaded{k}") for k in range(NBUF)]
        w1_hi_done, w1_lo_done = sem("w1_hi_done"), sem("w1_lo_done")
        xeT_ready, xe_hi_kept, xe_lo_kept = sem("xeT_ready"), sem("xe_hi_kept"), sem("xe_lo_kept")
        hid_ready, gelu_done = sem("hid_ready"), sem("gelu_done")
        hidT_ready, hidT_kept = sem("hidT_ready"), sem("hidT_kept")
        y3_ready, y3_kept = sem("y3_ready"), sem("y3_kept")
        stats3_done, rstd3_done, x3_done, pool_3, dve_3 = (
            sem("stats3_done"), sem("rstd3_done"), sem("x3_done"), sem("pool_3"), sem("dve_3"))
        out_written = [sem(f"out_written{k}") for k in range(4)]

        N_FIRST, N_OTHER, N_FFN = 2, 10, 1 + NFC
        N_POOL_CONST = 21
        N_DVE_CONST = 5

        block = ctx.enter_context(nc.Block())

        @block.sync
        def _(sp):
            def load_pair(p, k):
                sp.wait_ge(v_ready, 4 * p - 4)
                sp.dma_start(xT_sb[k][:], xT[:, bass.ds(2 * p * P, 2 * P)]).then_inc(xT_loaded[k], 16)

            def load_batch(i, u):
                b = 2 * i + u
                at_least(sp, qkv1_ready, b - 1)
                sp.dma_start(ctx_sb[u][:], ctxT[:, bass.ds(b * S2, S2)]).then_inc(ctx_loaded[u], 16)
                at_least(sp, y_kept, b - 1)
                sp.dma_start(x_sb[u][:], x[bass.ds(b * P, P), :]).then_inc(x_loaded[u], 16)

            for k in range(3):
                sp.dma_start(wqkv_sb[:, k * INNER:(k + 1) * INNER], w_qkv[:, k * INNER:(k + 1) * INNER]).then_inc(
                    w_loaded[k], 16)
                if k < 2:
                    sp.dma_start(xT_sb[k][:], xT[:, 2 * k * P:2 * (k + 1) * P]).then_inc(xT_loaded[k], 16)
            sp.dma_start(wg_sb[:], w_gates).then_inc(first_w, 16)
            sp.dma_start(wout_sb[:], w_out.rearrange("(c p) d -> p c d", p=P)).then_inc(first_w, 16)
            for u in range(2):
                sp.dma_start(ctx_sb[u][:], ctxT[:, u * S2:(u + 1) * S2]).then_inc(ctx_loaded[u], 16)
                sp.dma_start(x_sb[u][:], x[u * P:(u + 1) * P, :]).then_inc(x_loaded[u], 16)
            for dst, src in ((wq_sb, wq), (wk_sb, wk), (wv_sb, wv), (wo_sb, wo), (bq_sb, bq), (bk_sb, bk),
                             (wr_sb, Wr), (mask_sb, mask)):
                sp.dma_start(dst[:], src).then_inc(other_w, 16)
            sp.dma_start(bv_sb[:], bv.partition_broadcast(S2)).then_inc(other_w, 16)
            sp.dma_start(bo_sb[:], bo.partition_broadcast(P)).then_inc(other_w, 16)
            sp.dma_start(b_in[0][:], b1.rearrange("e (q f) -> (e q) f", q=P // NE)).then_inc(b_loaded, 16)
            sp.dma_start(b_in[1][:], b2.rearrange("e (q f) -> (e q) f", q=P // NE)).then_inc(b_loaded, 16)
            sp.dma_start(w1_sb[:, :].rearrange("p (e f) -> p e f", e=NE),
                         W1.rearrange("e d f -> d e f")).then_inc(ffn_w, 16)
            for c in range(NFC):
                sp.dma_start(w2_sb[:, c, :].rearrange("p (e d) -> p e d", e=NE),
                             W2[:, c * P:(c + 1) * P, :].rearrange("e p d -> p e d")).then_inc(ffn_w, 16)
            with sp.Fori(1, B // 4) as q:
                for k in range(2):
                    load_pair(2 * q + k, k)
                    load_batch(2 * q + k - 1, 0)
                    load_batch(2 * q + k - 1, 1)
            load_batch(B // 2 - 1, 0)
            load_batch(B // 2 - 1, 1)

            sp.wait_ge(b_split, 1)
            for w, dst in enumerate((b1_3, b2_3)):
                for k in range(3):
                    sp.dma_start(dst[k:k + 1, :], b_part[w][k][:]).then_inc(b_placed, 16)

            sp.wait_ge(pool_const, N_POOL_CONST)
            sp.dma_start(scratch[NE * REGION:NE * REGION + P, :], nobody_row[:, 0, :]).then_inc(tails_written, 16)
            sp.wait_ge(tail_done, 1)
            for e in range(NE):
                end = sp.value_load(tail_i[0:1, e:e + 1], min_val=0, max_val=NE * REGION - 2 * P)
                sp.dma_start(scratch[bass.ds(end, 2 * P), :].rearrange("(p k) d -> p k d", k=2),
                             nobody_row[:]).then_inc(tails_written, 16)

            sp.wait_ge(table_done, 1)
            sp.wait_ge(tails_written, 16 * (NE + 1))
            sp.wait_ge(scattered[0], 16 * (B // 2))
            sp.wait_ge(scattered[1], 16 * (B // 2))

            def load_tile(jj, k):
                j = NBUF * jj + k
                start = sp.value_load(row_at[0:1, bass.ds(j, 1)], min_val=0, max_val=NE * REGION)
                at_least(sp, stats3_done, j + 1 - NBUF)
                sp.dma_start(trow[k][:], scratch[bass.ds(start, P), :]).then_inc(trow_loaded[k], 16)

            for k in range(NBUF):
                load_tile(0, k)
            with sp.Fori(1, NT // NBUF) as jj:
                for k in range(NBUF):
                    load_tile(jj, k)
            for k in range(4):
                sp.wait_ge(out_written[k], 16 * (NT // 4))

        @block.gpsimd
        def _(pool):
            def select(out_ap, in_ap, pattern, op, base=0, cm=0, fill=0.0):
                return pool.affine_select(out=out_ap, in_=in_ap, pattern=pattern, compare_op=op,
                                          fill=fill, base=base, channel_multiplier=cm)

            count = [0]

            def const(ins):
                ins.then_inc(pool_const, 1)
                count[0] += 1

            def settle():
                pool.wait_ge(pool_const, count[0])

            for t in (ones, ident, before, head_rows):
                const(pool.memset(t[:], 1.0))
            const(pool.memset(v_exp[:], 0.0))
            const(pool.memset(half_neg[:], -0.5))
            const(pool.iota(falling[:], [[-1, NE]], base=NE, channel_multiplier=0,
                            allow_small_or_imprecise_dtypes=True))
            const(pool.iota(region_of[:], [[REGION, NE]], base=0, channel_multiplier=0,
                            allow_small_or_imprecise_dtypes=True))
            const(pool.iota(tile_no[:], [[1, NT + 1], [0, NE]], base=0, channel_multiplier=0,
                            allow_small_or_imprecise_dtypes=True))
            const(pool.memset(nobody_row[:], 0.0))
            for u in range(2):
                const(pool.memset(v1[u][:, :, DH:HEAD_W], 1.0))
                const(pool.memset(row[u][:], 0.0))
            settle()
            const(select(ident[:], ident[:], [[-1, P]], ALU.is_equal, cm=1))
            const(select(before[:], before[:], [[1, P]], ALU.is_gt, cm=-1))
            const(select(head_rows[:], head_rows[:], [[-XD, H]], ALU.is_ge, cm=1))
            const(pool.memset(nobody_row[:, :, TOKEN], NOBODY))
            for u in range(2):
                const(pool.iota(row[u][:, TOKEN:TOKEN + 1], [[0, 1]], base=(u - 2) * P, channel_multiplier=1,
                                allow_small_or_imprecise_dtypes=True))
            settle()
            const(select(head_rows[:], head_rows[:], [[XD, H]], ALU.is_ge, base=XD - 1, cm=-1))
            assert count[0] == N_POOL_CONST
            settle()

            def take_wait():
                pool.sem_inc(pool_passed, 1)

            def step(q, v):
                i, u = 2 * q + v // 2, v % 2
                n = 2 * i + u
                m, r = n - 1, n - 2

                def causal(g):
                    at_least(pool, exp_done, 4 * n + g + 1)
                    take_wait()
                    select(probs[g][:], probs[g][:], [[0, 4], [1, P]], ALU.is_ge, cm=-1).then_inc(causal_done, 1)

                def inverse_std(k, count):
                    at_least(pool, stats_done[k], count)
                    take_wait()
                    pool.tensor_scalar(var_eps[:, k:k + 1], mv[:, k, 1:2], EPS, None, ALU.add).then_inc(pool_ln[k], 1)
                    at_least(pool, pool_ln[k], count)
                    take_wait()
                    pool.tensor_tensor(rstd[:, k:k + 1], var_eps[:, k:k + 1], half_neg[:], ALU.pow).then_inc(
                        rstd_done[k], 1)

                if has(n, 1, B):
                    inverse_std(0, m + 1)
                    at_least(pool, x1_done, m + 1)
                    take_wait()
                    pool.tensor_tensor(x1_bo[1 - u][:], x1[1 - u][:], bo_sb[:], ALU.add).then_inc(x1_bo_done, 1)
                if has(n, 0, B - 1):
                    causal(0)
                    causal(1)
                    causal(2)
                    causal(3)
                if has(n, 2, B + 1):
                    inverse_std(1, r + 1)
                if has(n, 1, B):
                    at_least(pool, xrec_done, 2 * m + 1)
                    take_wait()
                    pool.tensor_tensor(logits[:, 0:H // 2, :], logits[:, 0:H // 2, :],
                                       xrec[:, 0:H // 2].unsqueeze(2).broadcast_to([P, H // 2, S2]),
                                       ALU.mult).then_inc(xnorm_done[0], 1)
                if has(n, 2, B + 1):
                    if isinstance(n, int) and n == B + 1:
                        pool.wait_ge(tails_written, 16 * (NE + 1))
                        take_wait()
                    at_least(pool, row_done, r + 1)
                    take_wait()
                    pool.indirect_dma_start(scratch[0:NE * REGION, :], bass.IndirectOffsetOnAxis(pos_i[u][:, 0:1], 0),
                                            row[u][:], None).then_inc(scattered[u], 16)

            pool.wait_ge(other_w, 16 * N_OTHER)
            run_steps(pool, step)


            def tile(jj, k):
                j = 4 * jj + k
                pool.wait_ge(stats3_done, j + 1)
                take_wait()
                pool.tensor_scalar(var3[:], mv3[k % 2][:, 1:2], EPS, None, ALU.add).then_inc(pool_3, 1)
                pool.wait_ge(pool_3, j + 1)
                take_wait()
                pool.tensor_tensor(rstd3[k % 2][:], var3[:], half_neg[:], ALU.pow).then_inc(rstd3_done, 1)
                pool.wait_ge(x3_done, j + 1)
                take_wait()
                pool.indirect_dma_start(out_rows, bass.IndirectOffsetOnAxis(tok_i[k][:, 0:1], 0), x3[k][:], None,
                                        bounds_check=B * P - 1, oob_is_err=False).then_inc(out_written[k], 16)

            with pool.Fori(0, NT // 4) as jj:
                for k in range(4):
                    tile(jj, k)

        @block.scalar
        def _(act):
            def upper_x(k, use):
                act.wait_ge(xT_loaded[k], 16 * use)
                nc.scalar.copy(x_hi[k][:], xT_sb[k][:]).then_inc(x_hi_done, 1)

            upper_x(0, 1)
            for k in range(3):
                act.wait_ge(w_loaded[k], 16)
                e = slice(k * INNER, (k + 1) * INNER)
                nc.scalar.copy(w_hi[:, e], wqkv_sb[:, e]).then_inc(w_hi_done, 1)

            def upper_w1(e):
                act.wait_ge(w_lo_done, 3)
                act.wait_ge(ffn_w, 16 * N_FFN)
                nc.scalar.copy(wqkv_sb[:, bass.ds(e * FF, FF)].bitcast(F32R), w1_sb[:, bass.ds(e * FF, FF)]).then_inc(
                    w1_hi_done, 1)

            def step(q, v):
                i, u = 2 * q + v // 2, v % 2
                n = 2 * i + u
                m, r = n - 1, n - 2

                def capped(g):
                    at_least(act, scores_ready, 4 * n + g + 1)
                    nc.scalar.activation(probs[g][:], ps[:, g % 2, :].rearrange("p (h i) -> p h i", h=4), ACT.Tanh,
                                         scale=1.0 / (DH ** 0.5 * SOFTCAP)).then_inc(tanh_done, 1)

                def exped(g):
                    act.wait_ge(tanh_done, 4 * n + g + 1)
                    nc.scalar.activation(probs[g][:], probs[g][:], ACT.Exp, scale=SOFTCAP).then_inc(exp_done, 1)

                def upper_next_x():
                    if u == 1 and has(n, -1, B - 5):
                        at_least(act, v_ready, 2 * (n + 1))
                        upper_x(v // 2, q + 2)

                if has(n, 0, B - 1):
                    capped(0)
                    capped(1)
                    exped(0)
                    exped(1)
                    upper_next_x()
                    at_least(act, gates_kept, n + 1)
                    nc.scalar.activation(gate_e[:], gate_z[:], ACT.Exp, scale=-1.0).then_inc(gate_exp_done, 1)
                    capped(2)
                    capped(3)
                    exped(2)
                    exped(3)

                def keep_v(half):
                    if has(n, -1, B - 2):
                        at_least(act, v_ready, 2 * (n + 1) + half + 1)
                        nc.scalar.copy(v1[1 - u][:, 8 * half:8 * half + 8, 0:DH],
                                       ps[:, 7, :].rearrange("p (h d) -> p h d", d=DH)).then_inc(v_kept, 1)

                if not has(n, 0, B - 1):
                    upper_next_x()
                if has(n, 1, B):
                    at_least(act, lowest_done, m + 1)
                    for h in range(H // 2):
                        if h == 3:
                            keep_v(0)
                        last = nc.scalar.activation(logits[:, h, :], logits[:, h, :], ACT.Exp,
                                                    bias=lowest[:, h:h + 1], scale=-1.0,
                                                    accum_out=xsum[:, h:h + 1])
                    last.then_inc(xexp_done, 1)
                else:
                    keep_v(0)
                if has(n, 0, B - 1):
                    for k in range(2):
                        at_least(act, attnT_ready, 2 * n + k + 1)
                        nc.scalar.copy(attnT[:, 4 * k:4 * k + 4, :],
                                       ps[:, k, :].rearrange("p (c i) -> p c i", c=4)).then_inc(attnT_kept, 1)
                keep_v(1)
                if has(n, 1, B):
                    at_least(act, shifted, m + 1)
                    nc.scalar.activation(logits[:, H // 2:H, :], logits[:, H // 2:H, :], ACT.Exp,
                                         scale=-1.0).then_inc(xexp_done, 1)
                    for g in range(2):
                        at_least(act, xpT_ready, 4 * m + g + 1)
                        nc.scalar.copy(xprobsT[:, 4 * g:4 * g + 4, :],
                                       ps[0:S2, 2 + g, :].rearrange("p (h i) -> p h i", h=4)).then_inc(xpT_kept, 1)
                if has(n, 2, B + 1):
                    at_least(act, one_hot_done, r + 1)
                    nc.scalar.activation(r_exp[:], r_low[:], ACT.Exp, accum_out=r_sum[:]).then_inc(r_exp_done, 1)
                if v == 1 and has(n, 1, B - 1):
                    upper_w1(q)

            act.wait_ge(pool_const, N_POOL_CONST)
            run_steps(act, step)

            def gelu(j, k):
                act.wait_ge(hid_ready, j + 1)
                nc.scalar.activation(hid[k % 2][:], ps[:, 2 + k % 2, :], ACT.Gelu).then_inc(gelu_done, 1)

            def keep_hidT(j, k):
                act.wait_ge(hidT_ready, j + 1)
                nc.scalar.copy(hidT[k % 2][:], ps[:, 4 + k % 2, :].rearrange("p (c i) -> p c i", c=NFC)).then_inc(
                    hidT_kept, 1)

            gelu(0, 0)
            for j in range(1, AHEAD):
                gelu(j, j)
                keep_hidT(j - 1, j - 1)

            def tiles(jj):
                for k in range(NBUF):
                    j = NBUF * jj + k
                    if has(j, 0, NT - 1 - AHEAD):
                        gelu(j + AHEAD, k + AHEAD)
                    if has(j, 0, NT - AHEAD):
                        keep_hidT(j + AHEAD - 1, k + AHEAD - 1)

            with act.Fori(0, NT // NBUF - 1) as jj:
                tiles(jj)
            tiles(NT // NBUF - 1)

        @block.vector
        def _(dve):
            S, X, R = Chain(dve, dve_s, 7), Chain(dve, dve_x, 2), Chain(dve, dve_r, 10)
            T = Chain(dve, dve_t, 10 + 11)

            def step(q, v):
                i, u = 2 * q + v // 2, v % 2
                n = 2 * i + u
                m, r = n - 1, n - 2
                has_s, has_x, has_r = has(n, 0, B - 1), has(n, 1, B), has(n, 2, B + 1)
                has_qk, has_v = has(n, -2, B - 3), has(n, -1, B - 2)
                S.start(n)
                X.start(m)
                R.start(r)

                def keep_qk(j):
                    if has_qk:
                        at_least(dve, qk_ready, 4 * (n + 2) + j + 1)
                        bank, dst = (2, 3, 6, 6)[j], (qT, kT)[u][1 - v // 2]
                        dve.tensor_copy(dst[:, 2 * j:2 * j + 2, :],
                                        ps[:, bank, :].rearrange("p (c t) -> p c t", c=2)).then_inc(qk_kept, 1)

                av_out = ps[:, 0:2, 0:4 * HEAD_W].rearrange("p g (k d) -> p g k d", d=HEAD_W)

                def over_sums(half):
                    at_least(dve, av_ready, 2 * n + half + 1)
                    S.mark(dve.reciprocal(rsum[:], av_out[:, :, :, DH]))

                def with_gates(half):
                    g = gate[:, 8 * half:8 * half + 8].rearrange("p (k g) -> p g k", g=2)
                    S.need()
                    S.mark(dve.tensor_tensor(rgate[:], rsum[:], g, ALU.mult))

                def normalise(half):
                    dst = attn[:, 512 * half:512 * half + 512].rearrange("p (k g d) -> p g k d", g=2, d=DH)
                    S.need()
                    dve.tensor_tensor(dst, av_out[:, :, :, 0:DH],
                                      rgate[:].unsqueeze(3).broadcast_to([P, 2, 4, DH]),
                                      ALU.mult).then_inc(attn_kept, 1)

                def masked(g):
                    at_least(dve, xscores_ready, 4 * m + g + 1)
                    dve.scalar_tensor_tensor(logits[:, 4 * g:4 * g + 4, :],
                                             ps[:, 2 + g, 0:4 * S2].rearrange("p (h k) -> p h k", h=4),
                                             -(XD ** -0.5), mask_sb[:].unsqueeze(1).broadcast_to([P, 4, S2]),
                                             ALU.mult, ALU.add).then_inc(xscores_kept, 1)

                def minimum(half):
                    heads = slice(8 * half, 8 * half + 8)
                    dve.wait_ge(xscores_kept, 4 * m + 2 * half + 2)
                    low = dve.tensor_reduce(lowest[:, heads], logits[:, heads, :], AX.X, ALU.min)
                    if half == 0:
                        low.then_inc(lowest_done, 1)
                    else:
                        X.mark(low)

                def shift():
                    heads = slice(H // 2, H)
                    X.need()
                    dve.tensor_tensor(logits[:, heads, :], logits[:, heads, :],
                                      lowest[:, heads].unsqueeze(2).broadcast_to([P, H // 2, S2]),
                                      ALU.subtract).then_inc(shifted, 1)

                def over_xsums(half):
                    heads = slice(8 * half, 8 * half + 8)
                    dve.wait_ge(xexp_done, 2 * m + half + 1)
                    if half == 1:
                        X.mark(dve.tensor_reduce(xsum[:, heads], logits[:, heads, :], AX.X, ALU.add))
                        X.need()
                    dve.reciprocal(xrec[:, heads], xsum[:, heads]).then_inc(xrec_done, 1)
                    if half == 1:
                        dve.wait_ge(xrec_done, 2 * m + 2)
                        dve.tensor_tensor(logits[:, heads, :], logits[:, heads, :],
                                          xrec[:, heads].unsqueeze(2).broadcast_to([P, H // 2, S2]),
                                          ALU.mult).then_inc(xnorm_done[1], 1)

                if has_r:
                    for g in (2, 3):
                        at_least(dve, xpT_ready, 4 * r + g + 1)
                        dve.tensor_copy(xprobsT[:, 4 * g:4 * g + 4, :],
                                        ps[0:S2, 2 + g, :].rearrange("p (h i) -> p h i", h=4)).then_inc(xpT_b_kept, 1)
                if has_x:
                    dve.wait_ge(rstd_done[0], m + 1)
                    dve.tensor_scalar(x1[1 - u][:], y1[:], mv[:, 0, 0:1], rstd[:, 0:1], ALU.subtract,
                                      ALU.mult).then_inc(x1_done, 1)
                keep_qk(0)
                keep_qk(1)
                if u == 1 and has(n, -1, B - 5):
                    lower_x(v // 2, i + 3)
                if has_r:
                    at_least(dve, xav_ready, r + 1)
                    dve.tensor_copy(xattnT[:], ps[:, 7, 0:P]).then_inc(xattnT_kept, 1)
                if has_x:
                    at_least(dve, x1T_ready, m + 1)
                    dve.tensor_copy(x1T[:], ps[:, 4, 0:P]).then_inc(x1T_kept, 1)
                keep_qk(2)
                if has_r:
                    at_least(dve, y2_ready, r + 1)
                    dve.wait_ge(x1_bo_done, r + 1)
                    dve.tensor_tensor(y2[:], ps[:, 5, 0:P], x1_bo[u][:], ALU.add).then_inc(y2_kept, 1)
                if has_s:
                    at_least(dve, gate_exp_done, n + 1)
                    S.mark(dve.tensor_scalar(gate_1[:], gate_e[:], 1.0, None, ALU.add))
                if has_x:
                    at_least(dve, qkv1_ready, m + 1)
                    dve.tensor_scalar(q1T[:], ps[:, 7, 0:P], bq_sb[:, 0:1], None, ALU.add)
                if has_s:
                    S.need()
                    S.mark(dve.reciprocal(gate[:], gate_1[:]))
                if has_x:
                    dve.scalar_tensor_tensor(k_exp[:], ps[:, 7, P:P + S2].unsqueeze(1).broadcast_to([P, 4, S2]),
                                             bk_sb[:, 0:1], in_group[:].unsqueeze(2).broadcast_to([P, 4, S2]),
                                             ALU.add, ALU.mult)
                    dve.tensor_tensor(v_diag, ps[0:S2, 7, 2 * P:3 * P].rearrange("p (c h d) -> p c h d", c=4, h=4),
                                      bv_sb[:, :].rearrange("p (c h d) -> p c h d", c=4, h=4),
                                      ALU.add).then_inc(qkv1_kept, 1)
                if has_r:
                    dve.wait_ge(y2_kept, r + 1)
                    R.link(dve.bn_stats(bn[:, 1, :], y2[:]))
                    dve.sem_inc(dve_passed, 1)
                    dve.bn_aggr(mv[:, 1, :], bn[:, 1, :]).then_inc(stats_done[1], 1)
                if has_s:
                    over_sums(0)
                    with_gates(0)
                    normalise(0)
                if has_r:
                    at_least(dve, rstd_done[1], r + 1)
                    at_least(dve, scattered[u], 16 * (i - 1))
                    dve.tensor_scalar(row[u][:, 0:P], y2[:], mv[:, 1, 0:1], rstd[:, 1:2], ALU.subtract,
                                      ALU.mult).then_inc(x2_done, 1)
                if has_x:
                    masked(0)
                    masked(1)
                    minimum(0)
                    masked(2)
                    masked(3)
                    minimum(1)
                if has_s:
                    over_sums(1)
                    with_gates(1)
                    normalise(1)
                if has_r:
                    at_least(dve, x2T_ready, r + 1)
                    dve.tensor_copy(x2T[:], ps[:, 4, 0:P]).then_inc(x2T_kept, 1)
                if has_x:
                    over_xsums(0)
                keep_qk(3)
                if has_r:
                    at_least(dve, router_ready, r + 1)
                    lg = ps[:, 5, 0:NE]
                    R.mark(dve.tensor_reduce(r_max[:], lg, AX.X, ALU.max))
                if has_x:
                    shift()
                if has_r:
                    R.need()
                    R.mark(dve.tensor_scalar(r_low[:], lg, r_max[:, 0:1], None, ALU.subtract))
                    R.mark(dve.scalar_tensor_tensor(r_key[:], lg, r_max[:, 0:1], falling[:], ALU.is_equal, ALU.mult))
                if has_r:
                    R.need()
                    R.mark(dve.tensor_reduce(r_first[:], r_key[:], AX.X, ALU.max))
                if has_v:
                    at_least(dve, gates_ready, n + 2)
                    dve.tensor_copy(gate_z[:], ps[:, 3, 0:H]).then_inc(gates_kept, 1)
                if has_r:
                    R.need()
                    dve.tensor_scalar(one_hot_b[:], falling[:], r_first[:, 0:1], None, ALU.is_equal)
                    dve.tensor_scalar(one_hot[:], falling[:], r_first[:, 0:1], None,
                                      ALU.is_equal).then_inc(one_hot_done, 1)
                if has_x:
                    over_xsums(1)
                    X.end()
                if has_r:
                    at_least(dve, place_ready, r + 1)
                    R.mark(dve.tensor_tensor(r_at[:], ps[:, 5, P:P + NE], placed[:], ALU.add))
                    R.need()
                    dve.tensor_tensor(placed[:], ps[:, 5, P + NE:P + 2 * NE], placed[:], ALU.add).then_inc(place_kept, 1)
                    dve.wait_ge(one_hot_done, r + 1)
                    R.mark(dve.tensor_tensor(r_pos[:], r_at[:], one_hot[:], ALU.mult))
                    R.mark(dve.tensor_scalar(row[u][:, TOKEN:TOKEN + 1], row[u][:, TOKEN:TOKEN + 1], 2.0 * P, None,
                                             ALU.add))
                    R.need()
                    R.mark(dve.tensor_reduce(pos_f[:], r_pos[:], AX.X, ALU.add))
                    R.need()
                    R.mark(dve.tensor_copy(pos_i[u][:], pos_f[:]))
                    dve.wait_ge(r_exp_done, r + 1)
                    R.need()
                    dve.reciprocal(row[u][:, PROB:PROB + 1], r_sum[:]).then_inc(row_done, 1)
                if isinstance(n, int) and n == B:
                    dve.wait_ge(place_kept, r + 1)
                    dve.tensor_copy(tail_i[:], placed[:]).then_inc(tail_done, 1)
                if has_s:
                    at_least(dve, y_ready, n + 1)
                    dve.wait_ge(x_loaded[u], 16 * (i + 1))
                    dve.tensor_tensor(y1[:], ps[:, 6, 0:P], x_sb[u][:], ALU.add).then_inc(y_kept, 1)
                    dve.wait_ge(y_kept, n + 1)
                    S.link(dve.bn_stats(bn[:, 0, :], y1[:]))
                    dve.sem_inc(dve_passed, 1)
                    dve.bn_aggr(mv[:, 0, :], bn[:, 0, :]).then_inc(stats_done[0], 1)
                    S.end()
                if v == 2 and has(n, 2, B - 1):
                    lower_w1(q)
                if has_r:
                    R.end()

            def lower_w1(e):
                dve.wait_ge(w1_hi_done, e + 1)
                part = w1_sb[:, bass.ds(e * FF, FF)]
                dve.tensor_tensor(part.bitcast(F32R), part, wqkv_sb[:, bass.ds(e * FF, FF)], ALU.subtract).then_inc(
                    w1_lo_done, 1)

            def lower_x(k, count):
                dve.wait_ge(x_hi_done, count)
                dve.tensor_tensor(x_lo[k][:], xT_sb[k][:], x_hi[k][:].bitcast(F32), ALU.subtract).then_inc(x_lo_done, 1)

            def split_biases():
                dve.wait_ge(b_loaded, 32)
                for w in range(2):
                    T.link(dve.tensor_copy(b_part[w][0][:], b_in[w][:]))
                    T.link(dve.tensor_tensor(b_rest[w][:], b_in[w][:], b_part[w][0][:], ALU.subtract))
                    T.link(dve.tensor_copy(b_part[w][1][:], b_rest[w][:]))
                    T.link(dve.tensor_tensor(b_rest[w][:], b_rest[w][:], b_part[w][1][:], ALU.subtract))
                    T.link(dve.tensor_copy(b_part[w][2][:], b_rest[w][:]))
                dve.memset(ones_3[:], 1.0).then_inc(b_split, 1)

            v_diag = bass.AP(v_exp[:].tensor, v_exp[:].offset, [list(v_exp[:].ap[0]), [P, 4], [32 + XD, 4], [1, XD]])
            T.start(0)
            lower_x(0, 1)
            for k in range(3):
                dve.wait_ge(w_hi_done, k + 1)
                e = slice(k * INNER, (k + 1) * INNER)
                dve.tensor_tensor(w_lo[:, e], wqkv_sb[:, e], w_hi[:, e].bitcast(F32), ALU.subtract).then_inc(w_lo_done, 1)

            def constants():
                dve.wait_ge(pool_const, N_POOL_CONST)
                dve.tensor_reduce(in_group[:], head_rows[:, :].rearrange("p (g k) -> p k g", g=4), AX.X,
                                  ALU.add).then_inc(dve_const, 1)
                dve.wait_ge(other_w, 16 * N_OTHER)
                dve.tensor_scalar(mask_sb[:], mask_sb[:], 1.0e9, None, ALU.mult).then_inc(dve_const, 1)
                dve.tensor_copy(before_b[:], before[:]).then_inc(dve_const, 1)
                dve.tensor_copy(ones_b[:], ones[:]).then_inc(dve_const, 1)
                dve.tensor_copy(placed[:], region_of[:]).then_inc(dve_const, 1)
                dve.wait_ge(dve_const, N_DVE_CONST)

            run_steps(dve, step, constants, split_biases)

            dve.wait_ge(place_kept, B)
            T.link(dve.tensor_tensor(n_rows[:], placed[:], region_of[:], ALU.subtract))
            T.link(dve.tensor_scalar(n_tiles_i[:], n_rows[:], P - 1.0, None, ALU.add))
            T.link(dve.tensor_scalar(n_tiles_i[:], n_tiles_i[:], P.bit_length() - 1, None, ALU.logical_shift_right))
            T.link(dve.tensor_copy(n_tiles[:], n_tiles_i[:]))
            T.mark(dve.tensor_scalar(jump[:], n_tiles[:], -float(P), float(REGION), ALU.mult, ALU.add))
            T.link(dve.tensor_tensor_scan(tile_end[:], ones[:, 0:NE], n_tiles[:], 0.0, ALU.mult, ALU.add))

            def over_tiles(t):
                return t[0:1, :].unsqueeze(1).broadcast_to([1, NT + 1, NE])

            T.link(dve.tensor_tensor(past[:], tile_no[:], over_tiles(tile_end), ALU.is_ge))
            T.link(dve.tensor_tensor(jumps[:], past[:], over_tiles(jump), ALU.mult))
            T.link(dve.tensor_reduce(t_jump[:], jumps[:], AX.X, ALU.add))
            T.link(dve.scalar_tensor_tensor(t_row[:], tile_no[:, :, 0], float(P), t_jump[:], ALU.mult, ALU.add))
            dve.tensor_scalar(row_at[:], t_row[:], float(NE * REGION), None, ALU.min).then_inc(table_done, 1)
            T.link(dve.tensor_reduce(t_exp[:], past[:], AX.X, ALU.add))
            dve.tensor_scalar(exp_at[:], t_exp[:], NE - 1.0, float(P), ALU.min, ALU.mult).then_inc(table_done, 1)
            T.end()

            def keep_xeT(j, k):
                dve.wait_ge(xeT_ready, j + 1)
                at_least(dve, hid_ready, j - 1)
                dve.tensor_copy(xe_hi[k % 2][:], ps[:, k % 2, 0:P]).then_inc(xe_hi_kept, 1)
                dve.wait_ge(xe_hi_kept, j + 1)
                dve.tensor_tensor(xe_lo[k % 2][:], ps[:, k % 2, 0:P], xe_hi[k % 2][:].bitcast(F32),
                                  ALU.subtract).then_inc(xe_lo_kept, 1)

            def residual(j, k, use):
                dve.wait_ge(y3_ready, j + 1)
                at_least(dve, x3_done, j - 1)
                dve.scalar_tensor_tensor(y3[k % 2][:], ps[:, 6 + k % 2, 0:P], trow[k][:, PROB:PROB + 1],
                                         trow[k][:, 0:P], ALU.mult, ALU.add).then_inc(y3_kept, 1)
                at_least(dve, out_written[k % 4], 16 * use)
                dve.tensor_copy(tok_i[k % 4][:], trow[k][:, TOKEN:TOKEN + 1])
                dve.wait_ge(y3_kept, j + 1)
                dve.bn_stats(bn3[:], y3[k % 2][:]).then_inc(dve_3, 1)
                dve.wait_ge(dve_3, j + 1)
                dve.sem_inc(dve_passed, 1)
                dve.bn_aggr(mv3[k % 2][:], bn3[:]).then_inc(stats3_done, 1)

            def norm3(j, k):
                dve.wait_ge(rstd3_done, j + 1)
                dve.tensor_scalar(x3[k % 4][:], y3[k % 2][:], mv3[k % 2][:, 0:1], rstd3[k % 2][:, 0:1],
                                  ALU.subtract, ALU.mult).then_inc(x3_done, 1)

            def tiles(jj):
                for k in range(NBUF):
                    j = NBUF * jj + k
                    if has(j, 0, NT - 1 - AHEAD):
                        keep_xeT(j + AHEAD, k + AHEAD)
                    residual(j, k, 2 * jj + k // 4)
                    if has(j, 1, NT):
                        norm3(j - 1, k - 1)

            for j in range(AHEAD):
                keep_xeT(j, j)
            tiles(0)
            with dve.Fori(1, NT // NBUF - 1) as jj:
                tiles(jj)
            tiles(NT // NBUF - 1)
            norm3(NT - 1, NBUF - 1)

        @block.tensor
        def _(pe):
            mm, tr = pe.matmul, pe.transpose

            def step(q, v):
                i, u = 2 * q + v // 2, v % 2
                n = 2 * i + u
                m, r = n - 1, n - 2
                has_s, has_x, has_r = has(n, 0, B - 1), has(n, 1, B), has(n, 2, B + 1)
                has_qk, has_v = has(n, -2, B - 3), has(n, -1, B - 2)

                def scores(g):
                    if g == 0:
                        at_least(pe, qk_kept, 4 * min(n + 2, B) if isinstance(n, int) else 4 * (n + 2))
                        at_least(pe, attnT_kept, 2 * n)
                    else:
                        at_least(pe, tanh_done, 4 * n + 2)
                    for k in range(4):
                        for w in range(2):
                            h = head_of(g + w, k)
                            rows = slice(DH * (h % 2), DH * (h % 2) + DH)
                            at = slice(u * P, (u + 1) * P)
                            last = mm(ps[:, w, k * P:(k + 1) * P], kT[v // 2][rows, h // 2, at],
                                      qT[v // 2][rows, h // 2, at],
                                      start=True, stop=True)
                            if k == 3:
                                last.then_inc(scores_ready, 1)

                pair = 1 - v // 2
                half_x = slice(P, 2 * P) if u == 0 else slice(0, P)
                next_x = v // 2 if u == 0 else pair
                parts = ((0, 0), (0, 1), (1, 0))
                xs, ws = (x_hi, x_lo), (w_hi, w_lo)

                def project_qk(j):
                    if not has_qk:
                        return
                    bank = (2, 3, 6, 6)[j]
                    if j == 0:
                        at_least(pe, x_lo_done, i + 2)
                        if isinstance(n, int) and n < 1:
                            pe.wait_ge(w_lo_done, 1 + u)
                        if isinstance(n, int) and n < 3:
                            at_least(pe, qk_kept, 4 * (n + 2))
                        at_least(pe, xpT_kept, 2 * (n - 2) + 1)
                    elif j == 1:
                        at_least(pe, gates_kept, n + 1)
                        at_least(pe, xpT_kept, 2 * (n - 2) + 2)
                    elif j == 2:
                        at_least(pe, y_kept, n)
                    elif j == 3:
                        at_least(pe, qk_kept, 4 * (n + 2) + 3)
                    for c in range(2):
                        e = u * INNER + (2 * j + c) * P
                        for t, (a, b) in enumerate(parts):
                            last = mm(ps[:, bank, c * 2 * P:(c + 1) * 2 * P], ws[a][:, e:e + P], xs[b][pair][:],
                                      start=(t == 0), stop=(t == 2))
                    last.then_inc(qk_ready, 1)

                def project_v(half, t):
                    if not has_v:
                        return
                    if half == 1 and t == 0:
                        at_least(pe, v_kept, 2 * (n + 1) + 1)
                    elif t == 0 and isinstance(n, int) and n < 3:
                        pe.wait_ge(w_lo_done, 3)
                        at_least(pe, v_kept, 2 * (n + 1))
                    e = 2 * INNER + 512 * half
                    a, b = parts[t]
                    last = mm(ps[:, 7, :], xs[b][next_x][:, half_x], ws[a][:, e:e + 512], start=(t == 0), stop=(t == 2))
                    if t == 2:
                        last.then_inc(v_ready, 1)

                def weigh(half):
                    if half == 0:
                        at_least(pe, tanh_done, 4 * n + 4)
                        at_least(pe, v_kept, 2 * (n + 1))
                    else:
                        at_least(pe, attn_kept, 2 * n + 1)
                    for w in range(2):
                        g = 2 * half + w
                        at_least(pe, causal_done, 4 * n + g + 1)
                        for k in range(4):
                            last = mm(ps[:, w, k * HEAD_W:(k + 1) * HEAD_W], probs[g][:, k, :],
                                      v1[u][:, head_of(g, k), :], start=True, stop=True)
                    last.then_inc(av_ready, 1)

                def project_out(half):
                    at_least(pe, attnT_kept, 2 * n + half + 1)
                    if has_qk:
                        at_least(pe, qk_kept, 4 * (n + 3))
                    for c in range(4 * half, 4 * half + 4):
                        last = mm(ps[:, 6, 0:P], attnT[:, c, :], wout_sb[:, c, :], start=(c == 0),
                                  stop=(c == NCH - 1))
                    if half:
                        last.then_inc(y_ready, 1)

                def transpose_probs(half, b):
                    at_least(pe, xnorm_done[half], b + 1)
                    for g in (2 * half, 2 * half + 1):
                        at_least(pe, xscores_kept, 4 * b + g + 1)
                        for k in range(4):
                            last = tr(ps[0:S2, 2 + g, k * P:(k + 1) * P], logits[:, 4 * g + k, :], ident[:])
                        last.then_inc(xpT_ready, 1)

                if has_s:
                    scores(0)
                if has_r:
                    at_least(pe, x2T_kept, r)
                    at_least(pe, place_kept, r)
                    transpose_probs(1, r)
                project_qk(0)
                project_qk(1)
                if has_s:
                    scores(2)
                if has_r:
                    at_least(pe, xpT_kept, 2 * (r + 1))
                    at_least(pe, xpT_b_kept, 2 * (r + 1))
                    at_least(pe, v_kept, 2 * min(n + 1, B))
                    for k in range(4):
                        for c in range(4):
                            last = mm(ps[32 * c:32 * c + 32, 7, 0:P], v_exp[:, 4 * c + k, :],
                                      xprobsT[:, 4 * c + k, :], start=(k == 0), stop=(k == 3))
                    last.then_inc(xav_ready, 1)
                if has_x:
                    at_least(pe, xpT_b_kept, 2 * (n - 2) + 1)
                    at_least(pe, x1_done, m + 1)
                    tr(ps[:, 4, 0:P], x1[1 - u][:], ident[:]).then_inc(x1T_ready, 1)
                project_qk(2)
                if has_r:
                    at_least(pe, xattnT_kept, r + 1)
                    mm(ps[:, 5, 0:P], xattnT[:], wo_sb[:], start=True, stop=True).then_inc(y2_ready, 1)
                if has_x:
                    at_least(pe, v_kept, 2 * min(n + 1, B))
                    at_least(pe, xattnT_kept, n - 1)
                    at_least(pe, x1T_kept, m + 1)
                    at_least(pe, ctx_loaded[1 - u], 16 * (i + u))
                    mm(ps[:, 7, 0:P], wq_sb[:], x1T[:], start=True, stop=True)
                    mm(ps[:, 7, P:P + S2], wk_sb[:], ctx_sb[1 - u][:], start=True, stop=True)
                    mm(ps[0:S2, 7, 2 * P:3 * P], ctx_sb[1 - u][:], wv_sb[:], start=True,
                       stop=True).then_inc(qkv1_ready, 1)
                if has_s:
                    weigh(0)
                if has_x:
                    at_least(pe, qkv1_kept, m + 1)
                for g in range(4):
                    if has_x:
                        if has_qk and g < 2:
                            at_least(pe, qk_kept, 4 * (n + 2) + g + 1)
                        elif g == 3:
                            at_least(pe, y2_kept, n - 1)
                        elif g == 0:
                            at_least(pe, xpT_kept, 2 * (n - 2) + 1)
                        elif g == 1:
                            at_least(pe, xpT_kept, 2 * (n - 2) + 2)
                            at_least(pe, gates_kept, min(n + 1, B))
                        rows = slice(32 * g, 32 * g + 32)
                        mm(ps[:, 2 + g, 0:4 * S2], q1T[rows, :], k_exp[rows, :, :].rearrange("p h k -> p (h k)"),
                           start=True, stop=True).then_inc(xscores_ready, 1)
                    if g < 3:
                        project_v(0, g)
                if has_s:
                    weigh(1)
                if has_r:
                    at_least(pe, x2_done, r + 1)
                    at_least(pe, xpT_b_kept, 2 * (r + 1))
                    if has_x:
                        at_least(pe, xscores_kept, 4 * m + 3)
                    tr(ps[:, 4, 0:P], row[u][:, 0:P], ident[:]).then_inc(x2T_ready, 1)
                project_qk(3)
                if has_v:
                    if has_x:
                        at_least(pe, xscores_kept, 4 * m + 2)
                    else:
                        at_least(pe, qk_kept, 4 * (n + 2) + 2)
                    if isinstance(n, int) and n < 0:
                        pe.wait_ge(first_w, 16 * N_FIRST)
                    mm(ps[:, 3, 0:H], xT_sb[next_x][:, half_x], wg_sb[:], start=True, stop=True).then_inc(gates_ready, 1)
                project_v(1, 0)
                project_v(1, 1)
                if has_s:
                    at_least(pe, attn_kept, 2 * n + 2)
                    for w in range(2):
                        for c in range(4):
                            last = tr(ps[:, w, c * P:(c + 1) * P], attn[:, (4 * w + c) * P:(4 * w + c + 1) * P],
                                      ident[:])
                        last.then_inc(attnT_ready, 1)
                if has_r:
                    at_least(pe, x2T_kept, r + 1)
                    if has_x:
                        at_least(pe, xscores_kept, 4 * m + 4)
                    mm(ps[:, 5, 0:NE], x2T[:], wr_sb[:], start=True, stop=True).then_inc(router_ready, 1)
                project_v(1, 2)
                if has_s:
                    project_out(0)
                    project_out(1)
                if has_x:
                    if has_v:
                        at_least(pe, gates_kept, n + 2)
                    transpose_probs(0, m)
                if has_r:
                    at_least(pe, one_hot_done, r + 1)
                    mm(ps[:, 5, P:P + NE], before_b[:], one_hot_b[:], start=True, stop=True)
                    mm(ps[:, 5, P + NE:P + 2 * NE], ones_b[:], one_hot_b[:], start=True,
                       stop=True).then_inc(place_ready, 1)

            def constants():
                pe.wait_ge(pool_const, N_POOL_CONST)
                pe.wait_ge(dve_const, N_DVE_CONST)
                pe.wait_ge(other_w, 16 * N_OTHER)

            run_steps(pe, step, constants)

            def T(j, k, jj):
                pe.wait_ge(trow_loaded[k % NBUF], 16 * (jj + k // NBUF + 1))
                tr(ps[:, k % 2, 0:P], trow[k % NBUF][:, 0:P], ident[:]).then_inc(xeT_ready, 1)

            def hidden(j, k, e):
                pe.wait_ge(xe_hi_kept, j + 1)
                w1_hi, w1_lo = (w[:, bass.ds(e * NFC, FF)].bitcast(F32R) for w in (wqkv_sb, w1_sb))
                mm(ps[:, 2 + k % 2, :], ones_3[:], b1_3[:, bass.ds(e * NFC, FF)], start=True, stop=False)
                mm(ps[:, 2 + k % 2, :], xe_hi[k % 2][:], w1_hi, start=False, stop=False)
                mm(ps[:, 2 + k % 2, :], xe_hi[k % 2][:], w1_lo, start=False, stop=False)
                pe.wait_ge(xe_lo_kept, j + 1)
                mm(ps[:, 2 + k % 2, :], xe_lo[k % 2][:], w1_hi, start=False, stop=True).then_inc(hid_ready, 1)

            def hidden_T(j, k):
                pe.wait_ge(gelu_done, j + 1)
                for c in range(NFC):
                    last = tr(ps[:, 4 + k % 2, c * P:(c + 1) * P], hid[k % 2][:, c * P:(c + 1) * P], ident[:])
                last.then_inc(hidT_ready, 1)

            def output(j, k, e):
                pe.wait_ge(hidT_kept, j + 1)
                at_least(pe, y3_kept, j - 1)
                mm(ps[:, 6 + k % 2, 0:P], ones_3[:], b2_3[:, bass.ds(e, P)], start=True, stop=False)
                for c in range(NFC):
                    last = mm(ps[:, 6 + k % 2, 0:P], hidT[k % 2][:, c, :], w2_sb[:, c, bass.ds(e, P)],
                              start=False, stop=(c == NFC - 1))
                last.then_inc(y3_ready, 1)

            def expert(j):
                return pe.value_load(exp_at[0:1, bass.ds(j, 1)], min_val=0, max_val=(NE - 1) * P)

            pe.wait_ge(ffn_w, 16 * N_FFN)
            pe.wait_ge(b_placed, 16 * 6)
            pe.wait_ge(w1_hi_done, NE)
            pe.wait_ge(w1_lo_done, NE)
            pe.wait_ge(table_done, 2)
            T(0, 0, 0)
            T(1, 1, 0)
            hidden(0, 0, expert(0))
            T(2, 2, 0)
            hidden(1, 1, expert(1))
            hidden_T(0, 0)
            hidden(2, 2, expert(2))
            hidden_T(1, 1)

            def tiles(jj):
                chosen = {0: expert(NBUF * jj)}
                for k in range(NBUF):
                    j = NBUF * jj + k
                    more = has(j, 0, NT - 1 - AHEAD)
                    if more:
                        T(j + AHEAD, k + AHEAD, jj)
                    output(j, k, chosen[k])
                    if more:
                        chosen[k + AHEAD] = expert(j + AHEAD)
                        hidden(j + AHEAD, k + AHEAD, chosen[k + AHEAD])
                    if k + 1 < AHEAD:
                        chosen[k + 1] = expert(j + 1)
                    if has(j, 0, NT - AHEAD):
                        hidden_T(j + AHEAD - 1, k + AHEAD - 1)

            tiles(0)
            with pe.Fori(1, NT // NBUF - 1) as jj:
                tiles(jj)
            tiles(NT // NBUF - 1)


_OUT = (B, P, P)


def kernel(x, ctx_1024, mask_1x1xSxS2_fk1, L0_attn_w_qkv, L0_attn_w_gates, L0_attn_w_out,
           L0_xattn_wq, L0_xattn_bq, L0_xattn_wk, L0_xattn_bk, L0_xattn_wv, L0_xattn_bv, L0_xattn_wo, L0_xattn_bo,
           L0_ffn_Wr, L0_ffn_W1, L0_ffn_b1, L0_ffn_W2, L0_ffn_b2):
    import numpy as np
    import concourse.bacc as bacc
    from concourse.bass_utils import run_bass_kernel_spmd

    x = np.asarray(x)
    ctx = np.asarray(ctx_1024)
    arrays = {
        "x": x.reshape(B * P, P),
        "xT": x.transpose(2, 0, 1).reshape(P, B * P),
        "ctxT": ctx.transpose(2, 0, 1).reshape(P, B * S2),
        "mask": np.asarray(mask_1x1xSxS2_fk1).reshape(P, S2),
        "w_qkv": L0_attn_w_qkv, "w_gates": L0_attn_w_gates, "w_out": L0_attn_w_out,
        "wq": L0_xattn_wq, "bq": np.asarray(L0_xattn_bq).reshape(P, 1),
        "wk": L0_xattn_wk, "bk": np.asarray(L0_xattn_bk).reshape(P, 1),
        "wv": L0_xattn_wv, "bv": L0_xattn_bv, "wo": L0_xattn_wo, "bo": L0_xattn_bo,
        "Wr": L0_ffn_Wr, "W1": L0_ffn_W1, "b1": L0_ffn_b1, "W2": L0_ffn_W2, "b2": L0_ffn_b2,
    }
    nc = bacc.Bacc("TRN2", target_bir_lowering=False, num_devices=1)
    args, ins = [], {}
    for name, a in arrays.items():
        a = np.ascontiguousarray(a)
        ins[f"in_{name}"] = a
        args.append(nc.dram_tensor(f"in_{name}", a.shape, mybir.dt.from_np(a.dtype), kind="ExternalInput").ap())
    out = nc.dram_tensor("out", _OUT, F32, kind="ExternalOutput").ap()
    decoder_layer(nc, *args, out)
    r = run_bass_kernel_spmd(nc, [ins], core_ids=[0])
    return r.results[0]["out"]
```
